# Optimizing a Trainium2 kernel written in Bass

```python
import numpy as np
import jax
import jax.numpy as jnp

def _softmax(x, axis=-1):
    return jax.nn.softmax(x, axis=axis)

def _gelu(x):
    return jax.nn.gelu(x, approximate=True)

def _silu(x):
    return jax.nn.silu(x)

def _sigmoid(x):
    return jax.nn.sigmoid(x)

def _layernorm(x, axis=-1, eps=1e-05):
    m = jnp.mean(x, axis=axis, keepdims=True)
    v = jnp.var(x, axis=axis, keepdims=True)
    return (x - m) / jnp.sqrt(v + eps)

def _scatter_add(tgt, idx, src, axis=0):
    return tgt.at[idx].add(src)

def _segment_sum(src, seg, n):
    return jax.ops.segment_sum(src, seg, n)
kernel_name = 'mk_adj_preln_d4_adj_r2_94820b'

def setup_inputs(seed: int=0):
    np.random.seed(seed)
    _w = jnp.asarray

    def _rec_inputs():
        import jax
        import jax.numpy as jnp
        _gk = jax.random.key(seed)
        x = -0.006082 + 1.001 * jax.random.normal(jax.random.fold_in(_gk, 1), (8192, 64), jnp.float32)
        _a = jax.random.bernoulli(jax.random.fold_in(_gk, 2), 0.000976562, (8192, 8192))
        adj = _a.astype(jnp.int32)
        return (x, adj)
    x, adj = _rec_inputs()

    def _L0_gnn_setup():
        import jax, jax.numpy as jnp
        import numpy as np
        ALPHA = 0.2
        NEG_INF = -9000000000000000.0
        key = jax.random.key(seed)
        k1, k2, k3, k4 = jax.random.split(key, 4)
        N, F_IN, F_OUT = (512, 64, 64)
        h = jax.random.normal(k1, (N, F_IN), dtype=jnp.float32)
        adj = jax.random.randint(k2, (N, N), 0, 2, dtype=jnp.int32)
        lim_W = 1.414 * np.sqrt(6.0 / (F_IN + F_OUT))
        W = jax.random.uniform(k3, (F_IN, F_OUT), minval=-lim_W, maxval=lim_W, dtype=jnp.float32)
        lim_a = 1.414 * np.sqrt(6.0 / (2 * F_OUT + 1))
        a = jax.random.uniform(k4, (2 * F_OUT, 1), minval=-lim_a, maxval=lim_a, dtype=jnp.float32)
        return {'h': h, 'adj': adj, 'W': W, 'a': a}
    _L0_gnn_all = _L0_gnn_setup()
    _L0_gnn_in = {k: v for k, v in _L0_gnn_all.items() if k in ('W', 'a')}
    del _L0_gnn_all

    def _L1_gnn_setup():
        import jax, jax.numpy as jnp
        import numpy as np
        ALPHA = 0.2
        NEG_BIG = jnp.float32(-9000000000000000.0)
        key = jax.random.key(seed)
        k1, k2, k3, k4 = jax.random.split(key, 4)
        N, F_IN, F_OUT = (4096, 64, 64)
        inputs = jax.random.normal(k1, (N, F_IN), dtype=jnp.float32)
        adj = jax.random.randint(k2, (N, N), 0, 2, dtype=jnp.int32)
        gain = 1.414
        lim_w = gain * np.sqrt(6.0 / (F_IN + F_OUT))
        W = jax.random.uniform(k3, (F_IN, F_OUT), dtype=jnp.float32, minval=-lim_w, maxval=lim_w)
        lim_a = gain * np.sqrt(6.0 / (2 * F_OUT + 1))
        a = jax.random.uniform(k4, (2 * F_OUT, 1), dtype=jnp.float32, minval=-lim_a, maxval=lim_a)
        return {'inputs': inputs, 'adj': adj, 'W': W, 'a': a}
    _L1_gnn_all = _L1_gnn_setup()
    _L1_gnn_in = {k: v for k, v in _L1_gnn_all.items() if k in ('W', 'a')}
    del _L1_gnn_all

    def _L2_gnn_setup():
        import jax, jax.numpy as jnp
        import numpy as np
        N = 8192
        D = 64
        key = jax.random.key(seed)
        kx, ka = jax.random.split(key)
        x = jax.random.normal(kx, (N, D), dtype=jnp.float32)
        adj = jax.random.randint(ka, (N, N), 0, 2, dtype=jnp.int32)
        return {'x': x, 'adj': adj}
    _L2_gnn_all = _L2_gnn_setup()
    _L2_gnn_in = {k: v for k, v in _L2_gnn_all.items() if k in ()}
    del _L2_gnn_all

    def _L3_gnn_setup():
        import jax, jax.numpy as jnp
        import numpy as np
        N = 6144
        IN_C = 64
        OUT_C = 64
        NEG_INF = -1000000000.0
        key = jax.random.key(seed)
        k1, k2, k3, k4 = jax.random.split(key, 4)
        x = jax.random.normal(k1, (N, IN_C), dtype=jnp.float32)
        edge_index = jax.random.randint(k2, (N, N), 0, 2, dtype=jnp.int32)
        weight_w = jax.random.normal(k3, (IN_C, OUT_C), dtype=jnp.float32) * (1.0 / np.sqrt(IN_C))
        weight_a = jax.random.normal(k4, (2 * OUT_C, 1), dtype=jnp.float32) * (1.0 / np.sqrt(OUT_C))
        bias = jnp.zeros((OUT_C,), dtype=jnp.float32)
        return {'x': x, 'edge_index': edge_index, 'weight_w': weight_w, 'weight_a': weight_a, 'bias': bias}
    _L3_gnn_all = _L3_gnn_setup()
    _L3_gnn_in = {k: v for k, v in _L3_gnn_all.items() if k in ('weight_w', 'weight_a', 'bias')}
    del _L3_gnn_all
    return {'x': x, 'adj': adj, 'L0_gnn_W': _L0_gnn_in['W'], 'L0_gnn_a': _L0_gnn_in['a'], 'L1_gnn_W': _L1_gnn_in['W'], 'L1_gnn_a': _L1_gnn_in['a'], 'L3_gnn_weight_w': _L3_gnn_in['weight_w'], 'L3_gnn_weight_a': _L3_gnn_in['weight_a'], 'L3_gnn_bias': _L3_gnn_in['bias']}

def reference(x, adj, L0_gnn_W, L0_gnn_a, L1_gnn_W, L1_gnn_a, L3_gnn_weight_w, L3_gnn_weight_a, L3_gnn_bias):
    import jax
    import jax.numpy as jnp

    def _L0_gnn_ref(h, adj, W, a):
        import jax, jax.numpy as jnp
        import numpy as np
        ALPHA = 0.2
        NEG_INF = -9000000000000000.0
        F_OUT = W.shape[1]
        Wh = h @ W
        a1, a2 = (a[:F_OUT, 0], a[F_OUT:, 0])
        e = (Wh @ a1)[:, None] + (Wh @ a2)[None, :]
        e = jax.nn.leaky_relu(e, negative_slope=ALPHA)
        scores = jnp.where(adj > 0, e, jnp.float32(NEG_INF))
        attention = jax.nn.softmax(scores, axis=1)
        h_prime = attention @ Wh
        return jax.nn.elu(h_prime)

    def _L1_gnn_ref(inputs, adj, W, a):
        import jax, jax.numpy as jnp
        import numpy as np
        ALPHA = 0.2
        NEG_BIG = jnp.float32(-9000000000000000.0)
        Wh = inputs @ W
        F_out = W.shape[1]
        a_src = a[:F_out, 0]
        a_dst = a[F_out:, 0]
        e = (Wh @ a_src)[:, None] + (Wh @ a_dst)[None, :]
        e = jnp.where(e > 0, e, ALPHA * e)
        scores = jnp.where(adj > 0, e, NEG_BIG)
        attention = jax.nn.softmax(scores, axis=1)
        h_prime = attention @ Wh
        return jax.nn.elu(h_prime)

    def _L2_gnn_ref(x, adj):
        import jax, jax.numpy as jnp
        import numpy as np
        N = 8192
        D = 64
        a = (adj == 1).astype(x.dtype)
        return jnp.matmul(a, x) + x

    def _L3_gnn_ref(x, edge_index, weight_w, weight_a, bias):
        import jax, jax.numpy as jnp
        import numpy as np
        N = 6144
        IN_C = 64
        OUT_C = 64
        NEG_INF = -1000000000.0
        wh = x @ weight_w
        a_src = weight_a[:OUT_C, 0]
        a_dst = weight_a[OUT_C:, 0]
        e = (wh @ a_src)[:, None] + (wh @ a_dst)[None, :]
        e = jax.nn.leaky_relu(e, negative_slope=0.01)
        scores = jnp.where(edge_index > 0, e, NEG_INF)
        attention = jax.nn.softmax(scores, axis=1)
        out = attention @ wh
        return out + bias
    h = jnp.maximum(_layernorm(x, axis=-1), 0.0)
    x = x + _L0_gnn_ref(h, adj, L0_gnn_W, L0_gnn_a)
    h = jnp.maximum(_layernorm(x, axis=-1), 0.0)
    x = x + _L1_gnn_ref(h, adj, L1_gnn_W, L1_gnn_a)
    h = jnp.maximum(_layernorm(x, axis=-1), 0.0)
    x = x + _L2_gnn_ref(h, adj)
    h = jnp.maximum(_layernorm(x, axis=-1), 0.0)
    x = x + _L3_gnn_ref(h, adj, L3_gnn_weight_w, L3_gnn_weight_a, L3_gnn_bias)
    return x

_drawn_inputs = setup_inputs


def setup_inputs(seed=0):
    import zlib

    import numpy as np

    out = dict(_drawn_inputs(seed))
    spreads = {'L3_gnn_bias': (0.0, 0.568)}
    factors = {'L3_gnn_weight_a': 7.463}
    for name, (base, spread) in spreads.items():
        noise = np.random.default_rng([zlib.crc32(name.encode()), seed]).standard_normal(out[name].shape)
        drawn = base * np.exp(spread * noise) if base else spread * noise
        out[name] = jnp.asarray(drawn.astype(out[name].dtype))
    for name, factor in factors.items():
        out[name] = (out[name] * factor).astype(out[name].dtype)
    return out
```

```python
from contextlib import ExitStack
from math import exp, factorial

import concourse.bass as bass
from concourse import mybir

f32 = mybir.dt.float32
i32 = mybir.dt.int32
ALU = mybir.AluOpType
ACT = mybir.ActivationFunctionType
AX = mybir.AxisListType

N = 8192
F = 64
P = 128
T = N // P
SEG = 512
NSEG = N // SEG
CAP = 24
W = F + 2
REC = CAP + 4
OWN, DEG, TWOS = CAP, CAP + 1, CAP + 2
EPS = 1e-5
PAD = 1e38
BIG = 3e38
EDGE_RATE = 1.0 / 1024

LOAD, GAT, SUM = "load", "gat", "sum"
PASSES = [(LOAD, None, False), (GAT, 0.2, True), (GAT, 0.2, True), (SUM, None, False), (GAT, 0.01, False)]
NEG_INF = [-9e15, -9e15, None, -1e9]


def degree_bounds():
    mean = N * EDGE_RATE
    pmf = [exp(-mean) * mean ** k / factorial(k) for k in range(60)]
    out = [CAP]
    for first in range(2 * P, N, 2 * P):
        for b in range(1, CAP + 1):
            above = N * sum(pmf[b + 1:])
            if above + 4 * above ** 0.5 + (3 if above < 9 else 0) <= first or b == CAP:
                out.append(b)
                break
    return out


def runs_of(bounds):
    runs, before = [], 0
    for u, b in enumerate(bounds):
        if runs and u not in (1, len(bounds) - 1) and runs[-1][2] == b:
            runs[-1][1] = u + 1
        else:
            runs.append([u, u + 1, b, before])
        before += b
    return [tuple(r) for r in runs]


BOUNDS = degree_bounds()
RUNS = [runs_of([1] * (T // 2))] + [runs_of(BOUNDS)] * 4
SLOTS = [T // 2] + [sum(BOUNDS)] * 4


class Steps:

    def __init__(self, eng, sem):
        self.eng, self.sem, self.base, self.at = eng, sem, 0, 0

    def link(self, ins, alone=False):
        self.at += 1
        ins.then_inc(self.sem, 1)
        self.eng.wait_ge(self.sem, self.base + self.at)
        if alone:
            self.eng.nop(nofuse=True)

    def total(self):
        return self.base + self.at

    def start(self, base):
        self.base, self.at = base, 0


def build(nc, x, adj, w0, a0, w1, a1, w3, a3, bias3, out):
    ctx = ExitStack()
    with ctx:
        def sb(name, shape, dt=f32):
            return ctx.enter_context(nc.sbuf_tensor(name, shape, dt))

        def ps(name, shape):
            return ctx.enter_context(nc.psum_tensor(name, shape, f32))

        def sem(name):
            return ctx.enter_context(nc.semaphore(name))

        records_d = nc.dram_tensor("records_d", [N, REC], i32).ap()
        tables = [nc.dram_tensor(f"table{q}", [N, F if q == 2 else W], f32).ap() for q in range(4)]
        dst_d = [nc.dram_tensor(f"dst{i}", [1, N], f32).ap() for i in range(4)]

        adj_in = [sb(f"adj_in{i}", [P, N], i32) for i in range(2)]
        keys = sb("keys", [P, N])
        colkey = sb("colkey", [P, N])
        X = sb("X", [P, T, F])
        H = sb("H", [P, T, W])
        top = sb("top", [P, T, CAP])
        rec = sb("rec", [P, T, REC], i32)
        srec = sb("srec", [P, T, REC], i32)
        cand = sb("cand", [P, NSEG, 8])
        left = sb("left", [P, NSEG, 8])
        seg8 = sb("seg8", [P, T])
        rest = sb("rest", [P, T])
        rest8 = sb("rest8", [P, 8])
        most = sb("most", [P, CAP])

        def carve(region, sizes):
            views, at = [], 0
            for shape, dt in sizes:
                n = 1
                for s in shape:
                    n *= s
                v = region[:, at:at + n].bitcast(dt) if region is not None else None
                if len(shape) == 2:
                    v = v.rearrange("p (a b) -> p a b", a=shape[0])
                elif len(shape) == 3:
                    v = v.rearrange("p (a b c) -> p a b c", a=shape[0], b=shape[1])
                views.append(v)
                at += n
            assert at <= N
            return views

        NV = CAP + 1
        is_v, run_v, zeros_v, is2, valid = carve(adj_in[0][:, :], [
            ((NV, T), f32), ((NV, T), f32), ((NV, T), f32), ((T, CAP), f32), ((T, CAP), f32)])
        key2, reci = carve(adj_in[1][:, :], [((T, CAP), f32), ((T, CAP), f32)])
        g0, g1, prod = carve(keys[:, :].bitcast(i32), [((CAP, W), f32), ((CAP, W), f32), ((CAP, F), f32)])
        gathered = [g0, g1]
        pad, once, sdeg = carve(colkey[:, :].bitcast(i32), [((T, CAP), f32), ((T, CAP), f32), ((T,), f32)])
        d_adj = adj_in[0]
        d_z = adj_in[1][:, :].bitcast(f32)
        d_t = keys
        d_dst = colkey

        ident = sb("ident", [P, P])
        ones = sb("ones", [P, P])
        lower = sb("lower", [P, P])
        own = sb("own", [P, T])
        slot = sb("slot", [P, CAP])
        degval = sb("degval", [P, NV])
        bound = sb("bound", [P, T])
        epsc = sb("epsc", [P, 1])
        wcat = [sb(f"wcat{i}", [F, W]) for i in range(3)]
        wT = [sb(f"wT{i}", [F, F]) for i in range(3)]
        acol = [sb(f"acol{i}", [F, 2]) for i in range(3)]
        biasb = sb("biasb", [P, F])
        deg = sb("deg", [P, T])
        nonempty = sb("nonempty", [P, T])
        empty = sb("empty", [P, T])
        cnt = sb("cnt", [P, NV])
        cpre = sb("cpre", [P, NV])
        tpre = sb("tpre", [P, NV])
        base_v = sb("base_v", [P, NV])
        zeros_s = sb("zeros_s", [P, NV])
        rank = sb("rank", [P, T], i32)
        over = sb("over", [P, T])
        over1 = sb("over1", [P, 1])
        flag = sb("flag", [1, 1], i32)
        ids = [sb(f"ids{i}", [P, CAP + 1], i32) for i in range(2)]
        pads = [sb(f"pads{i}", [P, CAP]) for i in range(2)]
        owns = [sb(f"owns{i}", [P, 1], i32) for i in range(2)]
        src = sb("src", [P, 2, T])
        score = [sb(f"score{i}", [P, CAP]) for i in range(2)]
        prob = [sb(f"prob{i}", [P, CAP]) for i in range(2)]
        nmax = [sb(f"nmax{i}", [P, 1]) for i in range(2)]
        rsum = [sb(f"rsum{i}", [P, 1]) for i in range(2)]
        rinv = sb("rinv", [P, 1])
        acc = [sb(f"acc{i}", [P, F]) for i in range(2)]
        fill = sb("fill", [P, F])
        hp = [sb(f"hp{i}", [P, F]) for i in range(2)]
        low = [sb(f"low{i}", [P, F]) for i in range(2)]
        ex = [sb(f"ex{i}", [P, F]) for i in range(2)]
        tmp = sb("tmp", [P, F])
        bn = sb("bn", [P, 6])
        mv = [sb(f"mv{i}", [P, 2]) for i in range(2)]
        lnv = [sb(f"lnv{i}", [P, 1]) for i in range(2)]
        rstd = [sb(f"rstd{i}", [P, 1]) for i in range(2)]
        hc = [sb(f"hc{i}", [P, F]) for i in range(2)]
        h = [sb(f"h{i}", [P, F]) for i in range(2)]
        hT = [sb(f"hT{i}", [F, P]) for i in range(2)]
        stage = [sb(f"stage{i}", [P, W]) for i in range(2)]
        whsum = sb("whsum", [P, W])
        meanb = sb("meanb", [P, F])
        zs = sb("zs", [P, 4 * P])
        zT = sb("zT", [P, 4 * P])

        ps_hT = [ps(f"ps_hT{i}", [F, P]) for i in range(2)]
        ps_wh = [ps(f"ps_wh{i}", [P, W]) for i in range(2)]
        ps_small = ps("ps_small", [P, 2 * W])
        ps_z = ps("ps_z", [P, 4 * P])
        ps_o = ps("ps_o", [P, F])

        adj_loaded = [sem(f"adj_loaded{i}") for i in range(2)]
        keyed = sem("keyed")
        colkey_ready = sem("colkey_ready")
        consts = sem("consts")
        params = sem("params")
        pool_step = sem("pool_step")
        dve_step = sem("dve_step")
        w_t = sem("w_t")
        w_tc = sem("w_tc")
        w_a = sem("w_a")
        w_ready = sem("w_ready")
        cnt_ready = sem("cnt_ready")
        cnt_summed = sem("cnt_summed")
        ranked = sem("ranked")
        scattered = sem("scattered")
        sorted_in = sem("sorted_in")
        over_ready = sem("over_ready")
        over_summed = sem("over_summed")
        flag_ready = sem("flag_ready")
        lists_ready = sem("lists_ready")
        ids_ready = sem("ids_ready")
        owns_ready = sem("owns_ready")
        gather_in = [sem(f"gather_in{i}") for i in range(2)]
        gather_free = sem("gather_free")
        table_out = [sem(f"table_out{i}") for i in range(2)]
        stage_ready = sem("stage_ready")
        score_ready = sem("score_ready")
        prob_ready = sem("prob_ready")
        low_ready = sem("low_ready")
        ex_ready = sem("ex_ready")
        var_ready = sem("var_ready")
        ln_ready = sem("ln_ready")
        rstd_ready = sem("rstd_ready")
        hc_ready = sem("hc_ready")
        h_ready = sem("h_ready")
        hT_psum = sem("hT_psum")
        hT_ready = sem("hT_ready")
        wh_psum = sem("wh_psum")
        whsum_ready = sem("whsum_ready")
        mean_psum = sem("mean_psum")
        d_x_in = sem("d_x_in")
        d_var = sem("d_var")
        d_ln = sem("d_ln")
        d_rstd = sem("d_rstd")
        d_hc = sem("d_hc")
        d_h = sem("d_h")
        d_hTp = sem("d_hTp")
        d_hT = sem("d_hT")
        d_whp = sem("d_whp")
        d_wh = sem("d_wh")
        d_dst_out = sem("d_dst_out")
        d_dst_in = sem("d_dst_in")
        d_adj_in = sem("d_adj_in")
        d_adj_free = sem("d_adj_free")
        d_z_ready = sem("d_z_ready")
        d_p_ready = sem("d_p_ready")
        d_zs = sem("d_zs")
        d_zTp = sem("d_zTp")
        d_zT = sem("d_zT")
        d_op = sem("d_op")
        d_acc = sem("d_acc")
        d_low = sem("d_low")
        d_ex = sem("d_ex")
        d_done = sem("d_done")
        d_out = sem("d_out")
        out_done = sem("out_done")

        dense_layers = [(GAT, 0.2, True, 0), (GAT, 0.2, True, 1), (SUM, None, False, None), (GAT, 0.01, False, 2)]

        def each_pair(eng, q, body):
            before = sum(SLOTS[:q])
            for u0, u1, slots, pre in RUNS[q]:
                if u1 - u0 == 1:
                    body(u0, slots, before + pre)
                else:
                    with eng.Fori(u0, u1) as u:
                        body(u, slots, before + pre + (u - u0) * slots)

        gat_no = {1: 0, 2: 1, 4: 2}
        prep_w = {0: 0, 1: 1, 3: 2}

        def row(t3, k):
            return t3[:, bass.ds(k, 1), :].rearrange("p a f -> p (a f)")

        def col(t2, k):
            return t2[:, bass.ds(k, 1)]

        block = ctx.enter_context(nc.Block())

        @block.sync
        def _(sp):
            def load_tile(t, i):
                sp.dma_start(adj_in[i][:, :], adj[bass.ds(t * P, P), :]).then_inc(adj_loaded[i], 16)

            load_tile(0, 0)
            load_tile(1, 1)
            for i, (w, a) in enumerate(((w0, a0), (w1, a1), (w3, a3))):
                sp.dma_start(wcat[i][:, 0:F], w).then_inc(params, 16)
                sp.dma_start(acol[i][:, 0:1], a[F:2 * F, :]).then_inc(params, 16)
                sp.dma_start(acol[i][:, 1:2], a[0:F, :]).then_inc(params, 16)
            sp.dma_start(biasb[:, :], bias3.rearrange("(a f) -> a f", a=1).broadcast_to((P, F))).then_inc(params, 16)
            with sp.Fori(1, T // 2) as u:
                for i in range(2):
                    sp.wait_ge(keyed, 2 * u + i - 1)
                    load_tile(2 * u + i, i)
            sp.wait_ge(scattered, 16 * T)
            sp.dma_start(srec[:, :, :], records_d.rearrange("(t p) c -> p t c", p=P)).then_inc(sorted_in, 16)

            sp.wait_ge(flag_ready, 1)
            dense = sp.value_load(flag[0:1, 0:1], min_val=0, max_val=1)
            with sp.If(dense > 0):
                sp.dma_start(X[:, :, :], x.rearrange("(t p) f -> p t f", p=P)).then_inc(d_x_in, 16)
                for n, (kind, _s, _e, _w) in enumerate(dense_layers):
                    if kind == GAT:
                        g = [0, 1, None, 2][n]
                        sp.wait_ge(d_wh, (n + 1) * T)
                        sp.dma_start(dst_d[n].rearrange("a (t p) -> p (a t)", p=P), H[:, :, F:F + 1].rearrange("p t a -> p (t a)"),
                                     allow_slow_non_contiguous=True).then_inc(d_dst_out, 16)
                        sp.wait_ge(d_dst_out, 16 * (g + 1))
                        sp.dma_start(d_dst[:, :], dst_d[n].broadcast_to((P, N))).then_inc(d_dst_in, 16)
                    with sp.Fori(0, T) as t:
                        sp.wait_ge(d_adj_free, n * (T + 1) + t + 1)
                        sp.dma_start(d_adj[:, :], adj[bass.ds(t * P, P), :]).then_inc(d_adj_in, 16)
                sp.wait_ge(d_done, 4 * T)
                sp.dma_start(out.rearrange("(t p) f -> p t f", p=P), X[:, :, :]).then_inc(d_out, 16)
                sp.wait_ge(d_out, 16)
            with sp.Else():
                sp.nop()

        @block.gpsimd
        def _(pool):
            steps = Steps(pool, pool_step)
            pool.iota(colkey[:, :], pattern=[[1, N]], base=N, channel_multiplier=0,
                      allow_small_or_imprecise_dtypes=True).then_inc(colkey_ready, 1)
            pool.memset(ident[:, :], 0.0).then_inc(pool_step, 1)
            pool.memset(ones[:, :], 1.0).then_inc(pool_step, 1)
            pool.memset(lower[:, :], 1.0).then_inc(pool_step, 1)
            pool.memset(epsc[:, :], EPS).then_inc(pool_step, 1)
            for u0, u1, b, _ in runs_of(BOUNDS):
                pool.memset(bound[:, 2 * u0:2 * u1], float(b)).then_inc(pool_step, 1)
            pool.iota(own[:, :], pattern=[[P, T]], base=0, channel_multiplier=1,
                      allow_small_or_imprecise_dtypes=True).then_inc(pool_step, 1)
            pool.iota(slot[:, :], pattern=[[1, CAP]], base=0, channel_multiplier=0,
                      allow_small_or_imprecise_dtypes=True).then_inc(pool_step, 1)
            pool.iota(degval[:, :], pattern=[[-1, NV]], base=CAP, channel_multiplier=0,
                      allow_small_or_imprecise_dtypes=True).then_inc(pool_step, 1)
            steps.at = 7 + len(runs_of(BOUNDS))
            pool.wait_ge(pool_step, steps.at)
            steps.link(pool.affine_select(out=ident[:, :], in_=ident[:, :], compare_op=ALU.not_equal, fill=1.0,
                                          base=0, pattern=[[-1, P]], channel_multiplier=1))
            steps.link(pool.affine_select(out=lower[:, :], in_=lower[:, :], compare_op=ALU.is_gt, fill=0.0,
                                          base=0, pattern=[[1, P]], channel_multiplier=-1))
            pool.sem_inc(consts, 1)

            pool.wait_ge(ranked, 1)
            for t in range(T):
                pool.indirect_dma_start(out=records_d, out_offset=bass.IndirectOffsetOnAxis(ap=rank[:, t:t + 1], axis=0),
                                        in_=rec[:, t, :], in_offset=None).then_inc(scattered, 16)
            pool.wait_ge(scattered, 16 * T)

            pool.wait_ge(flag_ready, 1)
            dense = pool.value_load(flag[0:1, 0:1], min_val=0, max_val=1)
            with pool.If(dense > 0):
                pool.nop()
            with pool.Else():
                def wait_then_dma(s, value):
                    pool.wait_ge(s, value)
                    pool.nop(nofuse=True)

                def put(q, k, i):
                    pool.wait_ge(owns_ready, T * q + k + 1)
                    wait_then_dma(stage_ready, T * q + k + 1)
                    dest = out if q == 4 else tables[q]
                    width = F if q in (2, 4) else W
                    pool.indirect_dma_start(out=dest, out_offset=bass.IndirectOffsetOnAxis(ap=owns[i][:, 0:1], axis=0),
                                            in_=stage[i][:, 0:width], in_offset=None).then_inc(table_out[i], 16)

                for q in range(5):
                    source = x if q == 0 else tables[q - 1]
                    width = F if q in (0, 3) else W
                    if q:
                        for i in range(2):
                            pool.wait_ge(table_out[i], 16 * q * (T // 2))

                    def pair(u, slots, _before, q=q, source=source, width=width):
                        for i in range(2):
                            k = 2 * u + i
                            pool.wait_ge(ids_ready, 2 * (T * q + k + 1))
                            if q or not isinstance(u, int) or u:
                                wait_then_dma(gather_free, T * q + k - 1)
                            for b in range(slots):
                                c = OWN if q == 0 else b
                                pool.indirect_dma_start(
                                    out=gathered[i][:, b, 0:width], out_offset=None, in_=source,
                                    in_offset=bass.IndirectOffsetOnAxis(ap=ids[i][:, c:c + 1], axis=0),
                                ).then_inc(gather_in[i], 16)
                            if not isinstance(u, int) or u:
                                put(q, k - 2, i)

                    each_pair(pool, q, pair)
                    for i in range(2):
                        put(q, T - 2 + i, i)
                for i in range(2):
                    pool.wait_ge(table_out[i], 16 * 5 * (T // 2))

        @block.vector
        def _(dve):
            v = nc.vector
            steps = Steps(dve, dve_step)
            dve.wait_ge(colkey_ready, 1)

            EXTRACT = 11

            def extract(u, first):
                for i in range(2):
                    t = 2 * u + i
                    steps.start(EXTRACT * t)
                    dve.wait_ge(adj_loaded[i], 16 * u + 16)
                    v.scalar_tensor_tensor(out=keys[:, :], in0=adj_in[i][:, :], scalar=2.0, in1=colkey[:, :],
                                           op0=ALU.min, op1=ALU.mult).then_inc(keyed, 1)
                    dve.wait_ge(keyed, t + 1)
                    dve.nop(nofuse=True)
                    for s in range(NSEG):
                        found = v.max(out=cand[:, s, :], in_=keys[:, s * SEG:(s + 1) * SEG])
                    steps.link(found)
                    steps.link(v.tensor_reduce(out=col(seg8, t), in_=cand[:, :, 7:8].rearrange("p s a -> p (s a)"),
                                               axis=AX.X, op=ALU.max), alone=True)
                    now = cand
                    for r in range(CAP // 8):
                        best = most[:, 8 * r:8 * r + 8]
                        steps.link(v.max(out=best, in_=now[:, :, :].rearrange("p s e -> p (s e)")), alone=True)
                        steps.link(v.match_replace(out=left[:, :, :].rearrange("p s e -> p (s e)"), in_to_replace=best,
                                                   in_values=now[:, :, :].rearrange("p s e -> p (s e)"), imm_value=0.0), alone=True)
                        now = left
                    steps.link(v.max(out=rest8[:, :], in_=left[:, :, :].rearrange("p s e -> p (s e)")))
                    v.tensor_copy(col(rest, t), rest8[:, 0:1]).then_inc(dve_step, 1)
                    steps.at += 1
                    steps.link(v.tensor_copy(row(top, t), most[:, :]))
                    assert steps.at == EXTRACT

            with dve.Fori(0, T // 2) as u:
                extract(u, False)
            steps.start(EXTRACT * T)
            dve.wait_ge(dve_step, EXTRACT * T)

            dve.wait_ge(consts, 1)
            link = steps.link
            keyv = top[:, :, :]
            ownb = own[:, :].unsqueeze(2).broadcast_to((P, T, CAP))
            link(v.tensor_scalar(is2, keyv, 2.0 * N, None, ALU.is_ge))
            link(v.tensor_scalar(valid, keyv, float(N), None, ALU.is_ge))
            link(v.scalar_tensor_tensor(out=key2, in0=is2, scalar=-0.5, in1=keyv, op0=ALU.mult, op1=ALU.mult))
            link(v.tensor_tensor(key2, key2, keyv, ALU.add))
            link(v.scalar_tensor_tensor(out=key2, in0=key2, scalar=-float(N), in1=ownb, op0=ALU.add, op1=ALU.subtract))
            link(v.tensor_tensor(key2, key2, valid, ALU.mult))
            link(v.tensor_tensor(rec[:, :, 0:CAP], key2, ownb, ALU.add))
            link(v.tensor_copy(rec[:, :, OWN], own[:, :]))
            link(v.tensor_reduce(out=deg[:, :], in_=valid, axis=AX.X, op=ALU.add))
            link(v.tensor_copy(rec[:, :, DEG], deg[:, :]))
            link(v.tensor_reduce(out=reci[:, :, 0], in_=is2, axis=AX.X, op=ALU.add))
            link(v.tensor_copy(rec[:, :, TWOS], reci[:, :, 0]))
            link(v.memset(rec[:, :, TWOS + 1], 0))
            link(v.memset(zeros_v, 0.0))
            link(v.memset(zeros_s[:, :], 0.0))
            link(v.tensor_tensor(is_v, deg[:, :].unsqueeze(1).broadcast_to((P, NV, T)),
                                 degval[:, :].unsqueeze(2).broadcast_to((P, NV, T)), ALU.is_equal))
            v.tensor_reduce(out=cnt[:, :], in_=is_v, axis=AX.X, op=ALU.add).then_inc(cnt_ready, 1)
            dve.wait_ge(cnt_ready, 1)
            flat = "p a b -> p (a b)"
            link(v.tensor_tensor_scan(run_v.rearrange(flat), is_v.rearrange(flat), zeros_v.rearrange(flat), 0.0,
                                      ALU.add, ALU.add))
            link(v.tensor_tensor_scan(cpre[:, :], cnt[:, :], zeros_s[:, :], 0.0, ALU.add, ALU.add))
            dve.wait_ge(cnt_summed, 1)
            link(v.tensor_tensor_scan(tpre[:, :], ps_small[:, W:W + NV], zeros_s[:, :], 0.0, ALU.add, ALU.add))
            link(v.tensor_tensor(tpre[:, :], tpre[:, :], ps_small[:, W:W + NV], ALU.subtract))
            link(v.tensor_tensor(cpre[:, :], cpre[:, :], cnt[:, :], ALU.subtract))
            link(v.tensor_tensor(base_v[:, :], tpre[:, :], ps_small[:, 0:NV], ALU.add))
            link(v.tensor_tensor(base_v[:, :], base_v[:, :], cpre[:, :], ALU.subtract))
            link(v.tensor_tensor(run_v, run_v, base_v[:, :].unsqueeze(2).broadcast_to((P, NV, T)), ALU.add))
            link(v.tensor_tensor(run_v, run_v, is_v, ALU.mult))
            link(v.tensor_reduce(out=reci[:, :, 1], in_=run_v.rearrange("p v t -> p t v"), axis=AX.X, op=ALU.add))
            v.tensor_scalar(rank[:, :], reci[:, :, 1], -1.0, None, ALU.add).then_inc(ranked, 1)

            dve.wait_ge(sorted_in, 16)
            link(v.tensor_copy(sdeg, srec[:, :, DEG]))
            slotb = slot[:, :].unsqueeze(1).broadcast_to((P, T, CAP))
            sdegb = sdeg.unsqueeze(2).broadcast_to((P, T, CAP))
            link(v.tensor_tensor(pad, slotb, sdegb, ALU.is_ge))
            link(v.tensor_copy(over[:, :], srec[:, :, TWOS]))
            link(v.tensor_tensor(once, slotb, over[:, :].unsqueeze(2).broadcast_to((P, T, CAP)), ALU.is_ge))
            link(v.tensor_tensor(once, once, pad, ALU.subtract))
            link(v.tensor_scalar(pad, pad, PAD, None, ALU.mult))
            link(v.tensor_scalar(nonempty[:, :], sdeg, 0.0, None, ALU.is_gt))
            link(v.tensor_scalar(empty[:, :], sdeg, 0.0, None, ALU.is_equal))
            link(v.tensor_tensor(over[:, :], sdeg, bound[:, :], ALU.is_gt))
            link(v.tensor_tensor(over[:, :], over[:, :], seg8[:, :], ALU.max))
            link(v.tensor_tensor(over[:, :], over[:, :], rest[:, :], ALU.max))
            v.tensor_reduce(out=over1[:, :], in_=over[:, :], axis=AX.X, op=ALU.max).then_inc(over_ready, 1)
            dve.wait_ge(over_summed, 1)
            v.tensor_scalar(flag[:, :], ps_small[0:1, 0:1], 0.0, None, ALU.is_gt).then_inc(flag_ready, 1)

            dve.wait_ge(flag_ready, 1)
            after_rank = steps.total()
            dense = dve.value_load(flag[0:1, 0:1], min_val=0, max_val=1)
            with dve.If(dense > 0):
                done = after_rank
                dve.wait_ge(d_x_in, 16)
                for n, (kind, slope, elu, wi) in enumerate(dense_layers):
                    g = [0, 1, None, 2][n]
                    PREP = 1
                    with dve.Fori(0, T) as t:
                        steps.start(done + PREP * t)
                        steps.link(v.bn_stats(out=bn[:, :], in_=row(X, t)), alone=True)
                        v.bn_aggr(out=mv[0][:, :], in_=bn[:, :]).then_inc(d_var, 1)
                        dve.wait_ge(d_rstd, n * T + t + 1)
                        v.tensor_scalar(hc[0][:, :], row(X, t), mv[0][:, 0:1], 0.0, ALU.subtract, ALU.max).then_inc(d_hc, 1)
                        if kind == GAT:
                            dve.wait_ge(d_whp, g * T + t + 1)
                            v.tensor_copy(row(H, t), ps_wh[0][:, :]).then_inc(d_wh, 1)
                        else:
                            dve.wait_ge(d_h, n * T + t + 1)
                            v.tensor_copy(row(H, t)[:, 0:F], h[0][:, :]).then_inc(d_wh, 1)
                        dve.wait_ge(d_wh, n * T + t + 1)
                        dve.nop(nofuse=True)
                        assert steps.at == PREP
                    done = done + PREP * T
                    if kind == GAT:
                        dve.wait_ge(d_dst_in, 16 * (g + 1))
                    dve.sem_inc(d_adj_free, 1)

                    ROWS = {0: 9, 1: 9, 2: 2, 3: 9}[n]
                    with dve.Fori(0, T) as t:
                        steps.start(done + ROWS * t)
                        dve.wait_ge(d_adj_in, 16 * (n * T + t + 1))
                        if kind == GAT:
                            link = steps.link
                            link(v.tensor_scalar(d_z, d_dst[:, :], row(H, t)[:, F + 1:F + 2], None, ALU.add))
                            link(v.scalar_tensor_tensor(out=d_z, in0=d_z, scalar=slope, in1=d_z, op0=ALU.mult, op1=ALU.max))
                            link(v.scalar_tensor_tensor(out=d_t[:, :], in0=d_adj[:, :], scalar=0.0, in1=d_z,
                                                        op0=ALU.is_gt, op1=ALU.mult))
                            v.tensor_scalar(d_z, d_adj[:, :], 0.0, NEG_INF[n], ALU.is_le, ALU.mult).then_inc(d_adj_free, 1)
                            dve.wait_ge(d_adj_free, n * (T + 1) + t + 2)
                            link(v.tensor_tensor(d_z, d_z, d_t[:, :], ALU.add))
                            link(v.tensor_reduce(out=nmax[1][:, :], in_=d_z, axis=AX.X, op=ALU.max))
                            v.tensor_scalar(nmax[0][:, :], nmax[1][:, :], -1.0, None, ALU.mult).then_inc(d_z_ready, 1)
                            dve.wait_ge(d_p_ready, g * T + t + 1)
                        else:
                            v.tensor_scalar(d_z, d_adj[:, :], 1.0, None, ALU.is_equal).then_inc(d_adj_free, 1)
                            dve.wait_ge(d_adj_free, n * (T + 1) + t + 2)
                            dve.sem_inc(d_z_ready, 1)
                        steps.link(v.memset(acc[0][:, :], 0.0), alone=True)
                        with dve.Fori(0, T // 4) as gr:
                            dve.wait_ge(d_op, (n * T + t) * (T // 4) + gr + 1)
                            v.tensor_tensor(acc[0][:, :], acc[0][:, :], ps_o[:, :], ALU.add).then_inc(d_acc, 1)
                            dve.wait_ge(d_acc, (n * T + t) * (T // 4) + gr + 1)
                            dve.nop(nofuse=True)
                        if kind == SUM:
                            steps.link(v.tensor_tensor(acc[0][:, :], acc[0][:, :], row(H, t)[:, 0:F], ALU.add))
                            v.tensor_tensor(row(X, t), row(X, t), acc[0][:, :], ALU.add).then_inc(d_done, 1)
                        else:
                            steps.link(v.reciprocal(rinv[:, :], rsum[0][:, :]))
                            steps.link(v.tensor_scalar(hp[0][:, :], acc[0][:, :], rinv[:, 0:1], None, ALU.mult))
                            if elu:
                                v.tensor_scalar(low[0][:, :], hp[0][:, :], 0.0, None, ALU.min).then_inc(d_low, 1)
                                dve.wait_ge(d_ex, g * T + t + 1)
                                steps.link(v.scalar_tensor_tensor(out=tmp[:, :], in0=hp[0][:, :], scalar=0.0, in1=ex[0][:, :],
                                                                  op0=ALU.max, op1=ALU.add))
                                v.scalar_tensor_tensor(out=row(X, t), in0=tmp[:, :], scalar=-1.0, in1=row(X, t),
                                                       op0=ALU.add, op1=ALU.add).then_inc(d_done, 1)
                            else:
                                steps.link(v.tensor_tensor(tmp[:, :], hp[0][:, :], biasb[:, :], ALU.add))
                                v.tensor_tensor(row(X, t), row(X, t), tmp[:, :], ALU.add).then_inc(d_done, 1)
                        dve.wait_ge(d_done, n * T + t + 1)
                        dve.nop(nofuse=True)
                        assert steps.at == ROWS, (n, steps.at)
                    done = done + ROWS * T
            with dve.Else():
                done = after_rank
                for q, (kind, slope, elu) in enumerate(PASSES):
                    g = gat_no.get(q)
                    last = q == 4
                    SCORES = 2 if kind == GAT else 0
                    ROWSUM = {GAT: 5, SUM: 1, LOAD: 0}[kind]
                    UPDATE = 1 if last else {GAT: 3, SUM: 3, LOAD: 1}[kind]
                    STORE = 0 if last else (1 if q == 2 else 2)
                    PER = SCORES + ROWSUM + UPDATE + STORE

                    def scores(q, k, i, slots):
                        g = gathered[i]
                        steps.link(v.tensor_scalar(score[i][:, 0:slots], g[:, 0:slots, F], -1.0,
                                                   src[:, (q - 1) % 2 if q < 3 else 1, bass.ds(k, 1)], ALU.mult, ALU.subtract))
                        steps.link(v.scalar_tensor_tensor(out=score[i][:, 0:slots], in0=score[i][:, 0:slots], scalar=slope,
                                                          in1=score[i][:, 0:slots], op0=ALU.mult, op1=ALU.min), alone=True)
                        v.tensor_tensor_reduce(out=score[i][:, 0:slots], in0=score[i][:, 0:slots],
                                               in1=pads[i][:, 0:slots], scale=1.0, scalar=BIG, op0=ALU.add,
                                               op1=ALU.min, accum_out=nmax[i][:, :]).then_inc(score_ready, 1)

                    def rowsum(q, k, i, slots):
                        g = gathered[i]
                        if kind == GAT:
                            dve.wait_ge(prob_ready, T * gat_no[q] + k + 1)
                            weight = prob[i][:, 0:slots]
                        else:
                            weight = row(once, k)[:, 0:slots]
                        v.tensor_tensor(prod[:, 0:slots, :], g[:, 0:slots, 0:F],
                                        weight.unsqueeze(2).broadcast_to((P, slots, F)), ALU.mult).then_inc(gather_free, 1)
                        dve.wait_ge(gather_free, T * q + k + 1)
                        steps.link(v.tensor_reduce(out=acc[i][:, :], in_=prod[:, 0:slots, :].rearrange("p b f -> p f b"),
                                                   axis=AX.X, op=ALU.add))
                        if kind == GAT:
                            steps.link(v.reciprocal(rinv[:, :], rsum[i][:, :]))
                            steps.link(v.tensor_tensor(rinv[:, :], rinv[:, :], col(nonempty, k), ALU.mult))
                            steps.link(v.tensor_scalar(fill[:, :], meanb[:, :], col(empty, k), None, ALU.mult))
                            steps.link(v.scalar_tensor_tensor(out=hp[i][:, :], in0=acc[i][:, :], scalar=rinv[:, 0:1],
                                                              in1=fill[:, :], op0=ALU.mult, op1=ALU.add))
                            if elu:
                                v.tensor_scalar(low[i][:, :], hp[i][:, :], 0.0, None, ALU.min).then_inc(low_ready, 1)

                    def update(q, k, i):
                        if kind == LOAD:
                            v.tensor_copy(row(X, k), gathered[i][:, 0, 0:F]).then_inc(gather_free, 1)
                            dve.wait_ge(gather_free, T * q + k + 1)
                        elif kind == SUM:
                            steps.link(v.tensor_tensor(tmp[:, :], acc[i][:, :], row(H, k)[:, 0:F], ALU.add))
                            steps.link(v.tensor_tensor(row(X, k), row(X, k), tmp[:, :], ALU.add))
                        elif elu:
                            dve.wait_ge(ex_ready, T * gat_no[q] + k + 1)
                            steps.link(v.scalar_tensor_tensor(out=tmp[:, :], in0=hp[i][:, :], scalar=0.0, in1=ex[i][:, :],
                                                              op0=ALU.max, op1=ALU.add))
                            steps.link(v.scalar_tensor_tensor(out=row(X, k), in0=tmp[:, :], scalar=-1.0, in1=row(X, k),
                                                              op0=ALU.add, op1=ALU.add))
                        else:
                            steps.link(v.tensor_tensor(tmp[:, :], hp[i][:, :], biasb[:, :], ALU.add))
                            dve.wait_ge(table_out[i], 16 * (T // 2 * q) + 16 * ((k - i) // 2) if isinstance(k, int)
                                        else 16 * (T // 2 * q) + 8 * (k - i))
                            v.tensor_tensor(stage[i][:, 0:F], row(X, k), tmp[:, :], ALU.add).then_inc(stage_ready, 1)
                        if not last:
                            dve.nop(nofuse=True)
                            steps.link(v.bn_stats(out=bn[:, :], in_=row(X, k)), alone=True)
                            v.bn_aggr(out=mv[i][:, :], in_=bn[:, :]).then_inc(var_ready, 1)
                            dve.wait_ge(var_ready, T * q + k + 1)
                            v.tensor_scalar(hc[i][:, :], row(X, k), mv[i][:, 0:1], 0.0, ALU.subtract, ALU.max).then_inc(hc_ready, 1)

                    def store(q, k, i):
                        if q or not isinstance(k, int) or k >= 2:
                            dve.wait_ge(table_out[i], 16 * (T // 2 * q) + 8 * (k - i))
                        if q == 2:
                            dve.wait_ge(h_ready, T * q + k + 1)
                            v.tensor_copy(stage[i][:, 0:F], h[i][:, :]).then_inc(stage_ready, 1)
                            steps.link(v.tensor_copy(row(H, k)[:, 0:F], h[i][:, :]))
                        else:
                            p = q if q < 2 else 2
                            dve.wait_ge(wh_psum, T * p + k + 1)
                            v.tensor_copy(stage[i][:, :], ps_wh[i][:, :]).then_inc(stage_ready, 1)
                            steps.link(v.tensor_copy(src[:, q % 2, bass.ds(k, 1)], ps_wh[i][:, F + 1:F + 2]))
                            if isinstance(k, int) and k == 0:
                                steps.link(v.tensor_copy(whsum[:, :], ps_wh[i][:, :]))
                            else:
                                steps.link(v.tensor_tensor(whsum[:, :], whsum[:, :], ps_wh[i][:, :], ALU.add))

                    def tile(q, k, i, slots, upto):
                        dve.wait_ge(gather_in[i], 16 * upto)
                        if kind == GAT:
                            scores(q, k, i, slots)
                        if not (isinstance(k, int) and k == 0):
                            update(q, k - 1, 1 - i)
                        if kind != LOAD:
                            rowsum(q, k, i, slots)
                        if not (isinstance(k, int) and k == 0) and not last:
                            store(q, k - 1, 1 - i)

                    def pair(u, slots, before):
                        for i in range(2):
                            k = 2 * u + i
                            if isinstance(k, int) and k == 0:
                                steps.start(done)
                                tile(q, k, i, slots, before + slots)
                                assert steps.at == PER - UPDATE - STORE, (q, steps.at)
                            else:
                                steps.start(done - UPDATE - STORE + PER * k)
                                tile(q, k, i, slots, before + slots)
                                assert steps.at == PER, (q, steps.at)

                    each_pair(dve, q, pair)
                    steps.start(done - UPDATE - STORE + PER * T)
                    update(q, T - 1, 1)
                    if not last:
                        store(q, T - 1, 1)
                    assert steps.at == UPDATE + STORE
                    done = done + PER * T
                    if q in prep_w:
                        dve.sem_inc(whsum_ready, 1)
                        dve.wait_ge(mean_psum, prep_w[q] + 1)
                        steps.start(done)
                        steps.link(v.tensor_scalar(meanb[:, :], ps_small[:, 0:F], 1.0 / N, None, ALU.mult))
                        done = done + 1

        @block.scalar
        def _(act):
            s = nc.scalar
            for i in range(3):
                act.wait_ge(w_t, i + 1)
                s.copy(wT[i][:, :], ps_hT[0][:, 0:F]).then_inc(w_tc, 1)
            for i in range(3):
                act.wait_ge(w_a, i + 1)
                s.copy(wcat[i][:, F:W], ps_hT[1][:, 0:2]).then_inc(w_ready, 1)

            act.wait_ge(flag_ready, 1)
            dense = act.value_load(flag[0:1, 0:1], min_val=0, max_val=1)

            with act.If(dense > 0):
                for n, (kind, _slope, elu, _w) in enumerate(dense_layers):
                    g = [0, 1, None, 2][n]
                    with act.Fori(0, T) as t:
                        act.wait_ge(d_var, n * T + t + 1)
                        s.activation(lnv[0][:, :], mv[0][:, 1:2], ACT.Ln, bias=epsc[:, 0:1]).then_inc(d_ln, 1)
                        act.wait_ge(d_ln, n * T + t + 1)
                        s.activation(rstd[0][:, :], lnv[0][:, :], ACT.Exp, scale=-0.5).then_inc(d_rstd, 1)
                        act.wait_ge(d_rstd, n * T + t + 1)
                        act.wait_ge(d_hc, n * T + t + 1)
                        s.activation(h[0][:, :], hc[0][:, :], ACT.Copy, scale=rstd[0][:, 0:1]).then_inc(d_h, 1)
                        if kind == GAT:
                            act.wait_ge(d_hTp, g * T + t + 1)
                            s.copy(hT[0][:, :], ps_hT[0][:, :]).then_inc(d_hT, 1)
                    with act.Fori(0, T) as t:
                        if kind == GAT:
                            act.wait_ge(d_z_ready, n * T + t + 1)
                            s.activation(d_z, d_z, ACT.Exp, bias=nmax[0][:, 0:1], accum_out=rsum[0][:, 0:1]).then_inc(d_p_ready, 1)
                            act.wait_ge(d_p_ready, g * T + t + 1)
                        else:
                            act.wait_ge(d_z_ready, n * T + t + 1)
                        with act.Fori(0, T // 4) as gr:
                            s.copy(zs[:, :], d_z[:, bass.ds(gr * (4 * P), 4 * P)]).then_inc(d_zs, 1)
                            act.wait_ge(d_zTp, (n * T + t) * (T // 4) + gr + 1)
                            s.copy(zT[:, :], ps_z[:, :]).then_inc(d_zT, 1)
                            act.wait_ge(d_acc, (n * T + t) * (T // 4) + gr + 1)
                        if elu:
                            act.wait_ge(d_low, g * T + t + 1)
                            s.activation(ex[0][:, :], low[0][:, :], ACT.Exp).then_inc(d_ex, 1)
            with act.Else():
                act.wait_ge(sorted_in, 16)

                def stage_ids(k, i):
                    s.copy(pads[i][:, :], row(pad, k)).then_inc(ids_ready, 1)
                    s.copy(ids[i][:, :], row(srec, k)[:, 0:CAP + 1]).then_inc(ids_ready, 1)

                stage_ids(0, 0)
                stage_ids(1, 1)
                for q, (kind, _slope, elu) in enumerate(PASSES):
                    last = q == 4

                    def normalise(q, k, i):
                        act.wait_ge(var_ready, T * q + k + 1)
                        s.activation(lnv[i][:, :], mv[i][:, 1:2], ACT.Ln, bias=epsc[:, 0:1]).then_inc(ln_ready, 1)
                        act.wait_ge(ln_ready, T * q + k + 1)
                        s.activation(rstd[i][:, :], lnv[i][:, :], ACT.Exp, scale=-0.5).then_inc(rstd_ready, 1)
                        act.wait_ge(rstd_ready, T * q + k + 1)
                        act.wait_ge(hc_ready, T * q + k + 1)
                        s.activation(h[i][:, :], hc[i][:, :], ACT.Copy, scale=rstd[i][:, 0:1]).then_inc(h_ready, 1)
                        if q != 2:
                            p = q if q < 2 else 2
                            act.wait_ge(hT_psum, T * p + k + 1)
                            s.copy(hT[i][:, :], ps_hT[i][:, :]).then_inc(hT_ready, 1)

                    def pair(u, slots, before, q=q, kind=kind, elu=elu, last=last):
                        for i in range(2):
                            k = 2 * u + i
                            start = isinstance(u, int) and u == 0
                            if kind == GAT:
                                act.wait_ge(score_ready, T * gat_no[q] + k + 1)
                                s.activation(prob[i][:, 0:slots], score[i][:, 0:slots], ACT.Exp, bias=nmax[i][:, 0:1],
                                             scale=-1.0, accum_out=rsum[i][:, 0:1]).then_inc(prob_ready, 1)
                            if not last and not (start and i == 0):
                                normalise(q, k - 1, 1 - i)
                            if elu:
                                act.wait_ge(low_ready, T * gat_no[q] + k + 1)
                                s.activation(ex[i][:, :], low[i][:, :], ACT.Exp).then_inc(ex_ready, 1)
                            if not (last and isinstance(u, int) and u == T // 2 - 1):
                                act.wait_ge(gather_in[i], 16 * (before + slots))
                                nxt = i if isinstance(u, int) and u == T // 2 - 1 else k + 2
                                stage_ids(nxt, i)
                            if q or not start:
                                act.wait_ge(table_out[i], 16 * (T // 2 * q + u))
                            s.copy(owns[i][:, :], row(srec, k)[:, OWN:OWN + 1]).then_inc(owns_ready, 1)

                    each_pair(act, q, pair)
                    if not last:
                        normalise(q, T - 1, 1)

        @block.tensor
        def _(pe):
            mm = nc.tensor.matmul
            pe.wait_ge(consts, 1)
            pe.wait_ge(params, 16 * 10)
            for i in range(3):
                if i:
                    pe.wait_ge(w_tc, i)
                nc.tensor.transpose(ps_hT[0][:, 0:F], wcat[i][:, 0:F], ident[0:F, 0:F]).then_inc(w_t, 1)
            for i in range(3):
                pe.wait_ge(w_tc, i + 1)
                if i:
                    pe.wait_ge(w_ready, i)
                mm(ps_hT[1][:, 0:2], wT[i][:, :], acol[i][:, :], start=True, stop=True).then_inc(w_a, 1)
            pe.wait_ge(cnt_ready, 1)
            mm(ps_small[:, 0:NV], lower[:, :], cnt[:, :], start=True, stop=True)
            mm(ps_small[:, W:W + NV], ones[:, :], cnt[:, :], start=True, stop=True).then_inc(cnt_summed, 1)
            pe.wait_ge(over_ready, 1)
            mm(ps_small[:, 0:1], ones[:, :], over1[:, :], start=True, stop=True).then_inc(over_summed, 1)
            pe.wait_ge(w_ready, 3)

            pe.wait_ge(flag_ready, 1)
            dense = pe.value_load(flag[0:1, 0:1], min_val=0, max_val=1)
            with pe.If(dense > 0):
                for n, (kind, _slope, _elu, wi) in enumerate(dense_layers):
                    g = [0, 1, None, 2][n]
                    if kind == GAT:
                        with pe.Fori(0, T) as t:
                            pe.wait_ge(d_h, n * T + t + 1)
                            pe.nop(nofuse=True)
                            nc.tensor.transpose(ps_hT[0][:, :], h[0][:, :], ident[:, :]).then_inc(d_hTp, 1)
                            pe.wait_ge(d_hT, g * T + t + 1)
                            mm(ps_wh[0][:, :], hT[0][:, :], wcat[wi][:, :], start=True, stop=True).then_inc(d_whp, 1)
                    with pe.Fori(0, T) as t:
                        with pe.Fori(0, T // 4) as gr:
                            now = (n * T + t) * (T // 4) + gr + 1
                            pe.wait_ge(d_zs, now)
                            for c in range(4):
                                tr = nc.tensor.transpose(ps_z[:, c * P:(c + 1) * P], zs[:, c * P:(c + 1) * P], ident[:, :])
                            tr.then_inc(d_zTp, 1)
                            pe.wait_ge(d_zT, now)
                            for c in range(4):
                                last = mm(ps_o[:, :], zT[:, c * P:(c + 1) * P],
                                          H[:, bass.ds(gr * 4 + c, 1), 0:F].rearrange("p a f -> p (a f)"),
                                          start=c == 0, stop=c == 3)
                            last.then_inc(d_op, 1)
            with pe.Else():
                for q in sorted(prep_w):
                    p = prep_w[q]
                    wi = p

                    def project(k, i, q=q, p=p, wi=wi):
                        pe.wait_ge(h_ready, T * q + k + 1)
                        pe.nop(nofuse=True)
                        nc.tensor.transpose(ps_hT[i][:, :], h[i][:, :], ident[:, :]).then_inc(hT_psum, 1)
                        pe.wait_ge(hT_ready, T * p + k + 1)
                        mm(ps_wh[i][:, :], hT[i][:, :], wcat[wi][:, :], start=True, stop=True).then_inc(wh_psum, 1)

                    with pe.Fori(0, T // 2) as u:
                        for i in range(2):
                            project(2 * u + i, i)
                    pe.wait_ge(whsum_ready, p + 1)
                    mm(ps_small[:, 0:F], ones[:, :], whsum[:, 0:F], start=True, stop=True).then_inc(mean_psum, 1)


_INS = ["x", "adj", "L0_gnn_W", "L0_gnn_a", "L1_gnn_W", "L1_gnn_a", "L3_gnn_weight_w", "L3_gnn_weight_a", "L3_gnn_bias"]


def kernel(**inputs):
    import numpy as np
    import concourse.bacc as bacc
    from concourse.bass_utils import run_bass_kernel_spmd

    nc = bacc.Bacc("TRN2", target_bir_lowering=False, num_devices=1)
    arrays, args = {}, []
    for name in _INS:
        a = np.ascontiguousarray(inputs[name])
        arrays[f"in_{name}"] = a
        args.append(nc.dram_tensor(f"in_{name}", a.shape, mybir.dt.from_np(a.dtype), kind="ExternalInput").ap())
    out = nc.dram_tensor("out_x", (N, F), f32, kind="ExternalOutput").ap()
    build(nc, *args, out)
    r = run_bass_kernel_spmd(nc, [arrays], core_ids=[0])
    return r.results[0]["out_x"]
```

```python
from contextlib import ExitStack
from math import exp, factorial

import concourse.bass as bass
from concourse import mybir

f32 = mybir.dt.float32
i32 = mybir.dt.int32
bf16 = mybir.dt.bfloat16
ALU = mybir.AluOpType
ACT = mybir.ActivationFunctionType
AX = mybir.AxisListType

N = 8192
F = 64
P = 128
T = N // P
FOLD = 8
FC = 512
WORDS = N // FOLD
SEG = 64
NSEG = WORDS // SEG
CAP = 24
W = F + 2
RANK = F + 1
OWN, DEG, SRC, MISS, FEAT = CAP, CAP + 1, CAP + 2, CAP + 3, CAP + 4
REC = FEAT + F
EPS = 1e-5
PAD = 1e38
BIG = 3e38
EDGE_RATE = 1.0 / 1024

GAT, SUM = "gat", "sum"
LAYERS = [(GAT, 0.2, True), (GAT, 0.2, True), (SUM, None, False), (GAT, 0.01, False)]
NEG_INF = [-9e15, -9e15, None, -1e9]


def degree_bounds():
    mean = N * EDGE_RATE
    pmf = [exp(-mean) * mean ** k / factorial(k) for k in range(60)]
    out = [CAP]
    for first in range(P, N, P):
        for b in range(1, CAP + 1):
            above = N * sum(pmf[b + 1:])
            if above + 4 * above ** 0.5 + (3 if above < 9 else 0) <= first or b == CAP:
                out.append(b)
                break
    return out


BOUNDS = degree_bounds()
SLOTS = [sum(BOUNDS[i::2]) for i in range(2)]


def pair_runs():
    runs, before = [], (0, 0)
    for u in range(T // 2):
        b = tuple(BOUNDS[2 * u:2 * u + 2])
        if runs and u not in (1, T // 2 - 1) and runs[-1][2] == b:
            runs[-1][1] = u + 1
        else:
            runs.append([u, u + 1, b, before])
        before = (before[0] + b[0], before[1] + b[1])
    return [tuple(r) for r in runs]


RUNS = pair_runs()


class Steps:

    def __init__(self, eng, sem):
        self.eng, self.sem, self.base, self.at = eng, sem, 0, 0

    def link(self, ins, alone=False):
        self.at += 1
        ins.then_inc(self.sem, 1)
        self.eng.wait_ge(self.sem, self.base + self.at)
        if alone:
            self.eng.nop(nofuse=True)

    def total(self):
        return self.base + self.at

    def start(self, base):
        self.base, self.at = base, 0


def build(nc, x, adj, w0, a0, w1, a1, w3, a3, bias3, out):
    ctx = ExitStack()
    with ctx:
        def sb(name, shape, dt=f32):
            return ctx.enter_context(nc.sbuf_tensor(name, shape, dt))

        def ps(name, shape):
            return ctx.enter_context(nc.psum_tensor(name, shape, f32))

        def sem(name):
            return ctx.enter_context(nc.semaphore(name))

        records_d = nc.dram_tensor("records_d", [N, REC], f32).ap()
        width = [F + 2, F + 1, F, F + 1]
        tables = [nc.dram_tensor(f"table{q}", [N, width[q]], f32).ap() for q in range(4)]
        dst_d = [nc.dram_tensor(f"dst{i}", [1, N], f32).ap() for i in range(4)]

        adj_in = [sb(f"adj_in{i}", [P, N], i32) for i in range(3)]
        adj_bf = sb("adj_bf", [P, 2, N], bf16)
        X = sb("X", [P, T, F])
        H = sb("H", [P, T, W])
        top = sb("top", [P, T, CAP])
        words = sb("words", [P, WORDS])
        colbase = sb("colbase", [P, 2, FC])
        cand = sb("cand", [P, NSEG, 8])
        left = sb("left", [P, NSEG, 8])
        most = sb("most", [P, 2, CAP])
        mosti = sb("mosti", [P, 2, CAP], i32)
        wordi = sb("wordi", [P, 2, CAP], i32)
        basei = sb("basei", [P, 2, CAP], i32)
        bitval = sb("bitval", [P, FOLD], i32)
        bitcol = sb("bitcol", [P, FOLD])
        bits = sb("bits", [P, 2, CAP, FOLD], i32)
        edge = sb("edge", [P, 2, CAP, FOLD])
        rest = sb("rest", [P, 2, CAP, FOLD])
        best = sb("best", [P, 2, CAP])
        total = sb("total", [P, T])
        diag = sb("diag", [P, FOLD, P], bf16)

        def carve(region, sizes):
            views, at = [], 0
            for shape in sizes:
                n = 1
                for m in shape:
                    n *= m
                v = region[:, at:at + n].bitcast(f32)
                if len(shape) == 2:
                    v = v.rearrange("p (a b) -> p a b", a=shape[0])
                views.append(v)
                at += n
            assert at <= N
            return views

        NV = CAP + 1
        x_nodes = H[:, :, 0:F]
        is_v, run_v, zeros_v, valid, nbr = carve(adj_in[0][:, :], [(NV, T), (NV, T), (NV, T), (T, CAP), (T, CAP)])
        g0, g1, prod = carve(adj_in[1][:, :], [(CAP, W), (CAP, W), (CAP, F)])
        gathered = [g0, g1]
        pad, once, sdeg, rec, srec = carve(adj_in[2][:, :], [(T, CAP), (T, CAP), (T,), (T, FEAT), (T, FEAT)])
        d_adj = adj_in[0]
        d_z = adj_in[1][:, :].bitcast(f32)
        d_t = adj_in[2][:, :].bitcast(f32)
        zs, zT = words[:, 0:4 * P], words[:, 4 * P:8 * P]
        d_dst = adj_bf[:, :, :].rearrange("p a n -> p (a n)").bitcast(f32)

        ident = sb("ident", [P, P])
        ones = sb("ones", [P, P])
        lower = sb("lower", [P, P])
        own = sb("own", [P, T])
        slot = sb("slot", [P, CAP])
        degval = sb("degval", [P, NV])
        bound = sb("bound", [P, T])
        epsc = sb("epsc", [P, 1])
        wcat = [sb(f"wcat{i}", [F, W]) for i in range(3)]
        wT = [sb(f"wT{i}", [F, F]) for i in range(3)]
        acol = [sb(f"acol{i}", [F, 2]) for i in range(3)]
        biasb = sb("biasb", [P, F])
        deg = sb("deg", [P, T])
        nonempty = sb("nonempty", [P, T])
        empty = sb("empty", [P, T])
        cnt = sb("cnt", [P, NV])
        cpre = sb("cpre", [P, NV])
        tpre = sb("tpre", [P, NV])
        base_v = sb("base_v", [P, NV])
        zeros_s = sb("zeros_s", [P, NV])
        rank = sb("rank", [P, T])
        rankv = sb("rankv", [P, T])
        recs = [sb(f"recs{i}", [P, REC]) for i in range(4)]
        places = [sb(f"places{i}", [P, 1], i32) for i in range(4)]
        over = sb("over", [P, T])
        over1 = sb("over1", [P, 1])
        flag = sb("flag", [1, 1], i32)
        ids = [sb(f"ids{i}", [P, CAP + 1], i32) for i in range(2)]
        pads = [sb(f"pads{i}", [P, CAP]) for i in range(2)]
        owns = [sb(f"owns{i}", [P, 1], i32) for i in range(2)]
        src = sb("src", [P, T])
        score = [sb(f"score{i}", [P, CAP]) for i in range(2)]
        prob = [sb(f"prob{i}", [P, CAP]) for i in range(2)]
        nmax = [sb(f"nmax{i}", [P, 1]) for i in range(2)]
        rsum = [sb(f"rsum{i}", [P, 1]) for i in range(2)]
        rinv = sb("rinv", [P, 1])
        acc = [sb(f"acc{i}", [P, F]) for i in range(2)]
        fill = sb("fill", [P, F])
        hp = [sb(f"hp{i}", [P, F]) for i in range(2)]
        low = [sb(f"low{i}", [P, F]) for i in range(2)]
        ex = [sb(f"ex{i}", [P, F]) for i in range(2)]
        tmp = sb("tmp", [P, F])
        bn = sb("bn", [P, 6])
        mv = [sb(f"mv{i}", [P, 2]) for i in range(2)]
        lnv = [sb(f"lnv{i}", [P, 1]) for i in range(2)]
        rstd = [sb(f"rstd{i}", [P, 1]) for i in range(2)]
        hc = [sb(f"hc{i}", [P, F]) for i in range(2)]
        h = [sb(f"h{i}", [P, F]) for i in range(2)]
        hT = [sb(f"hT{i}", [F, P]) for i in range(2)]
        stage = [sb(f"stage{i}", [P, W]) for i in range(2)]
        whsum = sb("whsum", [P, W])
        meanb = sb("meanb", [P, F])

        ps_hT_b = [ps(f"ps_hT_b{i}", [F, 4 * P]) for i in range(2)]
        ps_hT = [b[:, 0:P] for b in ps_hT_b]
        ps_wh_b = ps("ps_wh_b", [P, 4, P])
        ps_wh = [ps_wh_b[:, i, 0:W] for i in range(2)]
        ps_small_b = ps("ps_small_b", [P, 4 * P])
        ps_small = ps_small_b[:, 0:2 * W]
        ps_fold = [ps(f"ps_fold{i}", [P, 2, FC]) for i in range(2)]
        ps_z = ps_fold[0][:, 0, :]
        ps_o = ps_fold[1][:, 0, 0:F]

        x_loaded = sem("x_loaded")
        adj_loaded = [sem(f"adj_loaded{i}") for i in range(3)]
        narrowed = sem("narrowed")
        folded = sem("folded")
        worded = sem("worded")
        table0_out = [sem(f"table0_out{i}") for i in range(2)]
        rec_staged = sem("rec_staged")
        consts = sem("consts")
        params = sem("params")
        pool_step = sem("pool_step")
        dve_step = sem("dve_step")
        w_t = sem("w_t")
        w_tc = sem("w_tc")
        w_a = sem("w_a")
        w_ready = sem("w_ready")
        cnt_ready = sem("cnt_ready")
        cnt_summed = sem("cnt_summed")
        ranked = sem("ranked")
        scattered = [sem(f"scattered{i}") for i in range(4)]
        sorted_in = sem("sorted_in")
        over_ready = sem("over_ready")
        over_summed = sem("over_summed")
        flag_ready = sem("flag_ready")
        ids_ready = sem("ids_ready")
        owns_ready = sem("owns_ready")
        gather_in = [sem(f"gather_in{i}") for i in range(2)]
        gather_free = sem("gather_free")
        table_out = [sem(f"table_out{i}") for i in range(2)]
        rows_out = [sem(f"rows_out{i}") for i in range(2)]
        ranks_out = sem("ranks_out")
        stage_ready = sem("stage_ready")
        score_ready = sem("score_ready")
        prob_ready = sem("prob_ready")
        low_ready = sem("low_ready")
        ex_ready = sem("ex_ready")
        var_ready = sem("var_ready")
        ln_ready = sem("ln_ready")
        rstd_ready = sem("rstd_ready")
        hc_ready = sem("hc_ready")
        h_ready = sem("h_ready")
        hT_psum = sem("hT_psum")
        hT_ready = sem("hT_ready")
        wh_psum = sem("wh_psum")
        whsum_ready = sem("whsum_ready")
        mean_psum = sem("mean_psum")
        d_x_in = sem("d_x_in")
        d_var = sem("d_var")
        d_ln = sem("d_ln")
        d_rstd = sem("d_rstd")
        d_hc = sem("d_hc")
        d_h = sem("d_h")
        d_hTp = sem("d_hTp")
        d_hT = sem("d_hT")
        d_whp = sem("d_whp")
        d_wh = sem("d_wh")
        d_dst_out = sem("d_dst_out")
        d_dst_in = sem("d_dst_in")
        d_adj_in = sem("d_adj_in")
        d_adj_free = sem("d_adj_free")
        d_z_ready = sem("d_z_ready")
        d_p_ready = sem("d_p_ready")
        d_zs = sem("d_zs")
        d_zTp = sem("d_zTp")
        d_zT = sem("d_zT")
        d_op = sem("d_op")
        d_acc = sem("d_acc")
        d_low = sem("d_low")
        d_ex = sem("d_ex")
        d_done = sem("d_done")
        d_out = sem("d_out")
        out_done = sem("out_done")

        gat_no = {0: 0, 1: 1, 3: 2}
        weights = {0: 1, 2: 2}
        after = T

        def each_pair(eng, q, body):
            for u0, u1, slots, pre in RUNS:
                def run(u):
                    body(u, slots, [q * SLOTS[i] + pre[i] + (u - u0 + 1) * slots[i] for i in range(2)])
                if u1 - u0 == 1:
                    run(u0)
                else:
                    with eng.Fori(u0, u1) as u:
                        run(u)

        def row(t3, k):
            return t3[:, bass.ds(k, 1), :].rearrange("p a f -> p (a f)")

        def col(t2, k):
            return t2[:, bass.ds(k, 1)]

        def first(n):
            return isinstance(n, int) and n == 0

        def from_first(eng, end, body):
            body(0)
            with eng.Fori(1, end) as n:
                body(n)

        block = ctx.enter_context(nc.Block())

        @block.sync
        def _(sp):
            def load_tile(t, i):
                sp.dma_start(adj_in[i][:, :], adj[bass.ds(t * P, P), :]).then_inc(adj_loaded[i], 16)

            def store_tile(t, i):
                sp.wait_ge(stage_ready, t + 1)
                sp.dma_start(tables[0][bass.ds(t * P, P), 0:F + 1], stage[i][:, 0:F + 1]).then_inc(table0_out[i], 16)

            sp.dma_start(x_nodes, x.rearrange("(t p) f -> p t f", p=P)).then_inc(x_loaded, 16)
            for i, (w, a) in enumerate(((w0, a0), (w1, a1), (w3, a3))):
                sp.dma_start(wcat[i][:, 0:F], w).then_inc(params, 16)
                sp.dma_start(acol[i][:, 0:1], a[F:2 * F, :]).then_inc(params, 16)
                sp.dma_start(acol[i][:, 1:2], a[0:F, :]).then_inc(params, 16)
            for t in range(3):
                load_tile(t, t)
            sp.dma_start(biasb[:, :], bias3.rearrange("(a f) -> a f", a=1).broadcast_to((P, F))).then_inc(params, 16)
            def six(v6):
                for j in range(6):
                    t = 6 * v6 + j
                    sp.wait_ge(narrowed, t + 1)
                    load_tile(t + 3, j % 3)
                    if not first(v6) or j >= 2:
                        store_tile(t - 2, j % 2)

            from_first(sp, (T - 4) // 6, six)
            sp.wait_ge(narrowed, T - 3)
            load_tile(T - 1, (T - 1) % 3)
            for t in range(T - 6, T):
                store_tile(t, t % 2)
            for i in range(2):
                sp.wait_ge(table0_out[i], 16 * T // 2)
            sp.wait_ge(ranked, 1)
            sp.dma_start(tables[0].rearrange("(t p) c -> p t c", p=P)[:, :, RANK], rank[:, :],
                         allow_slow_non_contiguous=True).then_inc(ranks_out, 16)
            for i in range(4):
                sp.wait_ge(scattered[i], 16 * T // 4)
            ordered = records_d.rearrange("(t p) c -> p t c", p=P)
            sp.dma_start(srec, ordered[:, :, 0:FEAT]).then_inc(sorted_in, 16)
            sp.dma_start(X[:, :, :], ordered[:, :, FEAT:REC]).then_inc(sorted_in, 16)
            sp.wait_ge(ranks_out, 16)

            sp.wait_ge(flag_ready, 1)
            dense = sp.value_load(flag[0:1, 0:1], min_val=0, max_val=1)
            with sp.If(dense > 0):
                sp.dma_start(X[:, :, :], x.rearrange("(t p) f -> p t f", p=P)).then_inc(d_x_in, 16)
                for n, (kind, _slope, _elu) in enumerate(LAYERS):
                    if kind == GAT:
                        g = gat_no[n]
                        sp.wait_ge(d_wh, (n + 1) * T)
                        sp.dma_start(dst_d[n].rearrange("a (t p) -> p (a t)", p=P), H[:, :, F:F + 1].rearrange("p t a -> p (t a)"),
                                     allow_slow_non_contiguous=True).then_inc(d_dst_out, 16)
                        sp.wait_ge(d_dst_out, 16 * (g + 1))
                        sp.dma_start(d_dst, dst_d[n].broadcast_to((P, N))).then_inc(d_dst_in, 16)
                    with sp.Fori(0, T) as t:
                        sp.wait_ge(d_adj_free, n * (T + 1) + t + 1)
                        sp.dma_start(d_adj[:, :], adj[bass.ds(t * P, P), :]).then_inc(d_adj_in, 16)
                sp.wait_ge(d_done, 4 * T)
                sp.dma_start(out.rearrange("(t p) f -> p t f", p=P), X[:, :, :]).then_inc(d_out, 16)
                sp.wait_ge(d_out, 16)
            with sp.Else():
                for q in range(3):
                    def store_pair(u, q=q):
                        for i in range(2):
                            k = 2 * u + i
                            sp.wait_ge(stage_ready, after + T * q + k + 1)
                            sp.dma_start(tables[q + 1][bass.ds(k * P, P), :], stage[i][:, 0:width[q + 1]]).then_inc(table_out[i], 16)

                    with sp.Fori(0, T // 2) as u:
                        store_pair(u)
                for i in range(2):
                    sp.wait_ge(table_out[i], 16 * 3 * (T // 2))

        @block.gpsimd
        def _(pool):
            steps = Steps(pool, pool_step)
            pool.memset(ident[:, :], 0.0).then_inc(pool_step, 1)
            pool.memset(ones[:, :], 1.0).then_inc(pool_step, 1)
            pool.memset(lower[:, :], 1.0).then_inc(pool_step, 1)
            pool.memset(epsc[:, :], EPS).then_inc(pool_step, 1)
            for b in sorted(set(BOUNDS)):
                at = BOUNDS.index(b)
                pool.memset(bound[:, at:at + BOUNDS.count(b)], float(b)).then_inc(pool_step, 1)
            pool.iota(colbase[:, :, :], pattern=[[N // 2, 2], [1, FC]], base=0, channel_multiplier=0,
                      allow_small_or_imprecise_dtypes=True).then_inc(pool_step, 1)
            pool.iota(bitcol[:, :], pattern=[[FC, FOLD]], base=N, channel_multiplier=0,
                      allow_small_or_imprecise_dtypes=True).then_inc(pool_step, 1)
            for q in range(FOLD):
                pool.memset(bitval[:, q:q + 1], 1 << q).then_inc(pool_step, 1)
            pool.iota(own[:, :], pattern=[[P, T]], base=0, channel_multiplier=1,
                      allow_small_or_imprecise_dtypes=True).then_inc(pool_step, 1)
            pool.iota(slot[:, :], pattern=[[1, CAP]], base=0, channel_multiplier=0,
                      allow_small_or_imprecise_dtypes=True).then_inc(pool_step, 1)
            pool.iota(degval[:, :], pattern=[[-1, NV]], base=CAP, channel_multiplier=0,
                      allow_small_or_imprecise_dtypes=True).then_inc(pool_step, 1)
            steps.at = 9 + len(set(BOUNDS)) + FOLD
            pool.wait_ge(pool_step, steps.at)
            steps.link(pool.affine_select(out=ident[:, :], in_=ident[:, :], compare_op=ALU.not_equal, fill=1.0,
                                          base=0, pattern=[[-1, P]], channel_multiplier=1))
            for q in range(FOLD):
                steps.link(pool.tensor_scalar(diag[:, q, :], ident[:, :], float(1 << q), None, ALU.mult))
            steps.link(pool.affine_select(out=lower[:, :], in_=lower[:, :], compare_op=ALU.is_gt, fill=0.0,
                                          base=0, pattern=[[1, P]], channel_multiplier=-1))
            pool.sem_inc(consts, 1)

            with pool.Fori(0, T // 4) as t4:
                for i in range(4):
                    pool.wait_ge(rec_staged, 3 * (4 * t4 + i + 1))
                    pool.nop(nofuse=True)
                    pool.indirect_dma_start(out=records_d, out_offset=bass.IndirectOffsetOnAxis(ap=places[i][:, 0:1], axis=0),
                                            in_=recs[i][:, :], in_offset=None).then_inc(scattered[i], 16)
            for i in range(4):
                pool.wait_ge(scattered[i], 16 * T // 4)

            pool.wait_ge(flag_ready, 1)
            dense = pool.value_load(flag[0:1, 0:1], min_val=0, max_val=1)
            with pool.If(dense > 0):
                pool.nop()
            with pool.Else():
                def wait_then_dma(s, value):
                    pool.wait_ge(s, value)
                    pool.nop(nofuse=True)

                def put(k, i):
                    pool.wait_ge(owns_ready, k + 1)
                    wait_then_dma(stage_ready, after + T * 3 + k + 1)
                    pool.indirect_dma_start(out=out, out_offset=bass.IndirectOffsetOnAxis(ap=owns[i][:, 0:1], axis=0),
                                            in_=stage[i][:, 0:F], in_offset=None).then_inc(rows_out[i], 16)

                for i in range(2):
                    pool.wait_ge(table0_out[i], 16 * T // 2)
                pool.wait_ge(ranks_out, 16)
                for q in range(4):
                    if q:
                        for i in range(2):
                            pool.wait_ge(table_out[i], 16 * q * (T // 2))

                    def pair(u, slots, _upto, q=q):
                        for i in range(2):
                            k = 2 * u + i
                            pool.wait_ge(ids_ready, 2 * (T * q + k + 1))
                            if q or not isinstance(u, int) or u:
                                pool.wait_ge(gather_free, T * q + k - 1)
                            pool.nop(nofuse=True)
                            for b in range(slots[i]):
                                pool.indirect_dma_start(
                                    out=gathered[i][:, b, 0:width[q]], out_offset=None, in_=tables[q],
                                    in_offset=bass.IndirectOffsetOnAxis(ap=ids[i][:, b:b + 1], axis=0),
                                ).then_inc(gather_in[i], 16)
                            if q == 3 and not first(u):
                                put(k - 2, i)

                    each_pair(pool, q, pair)
                for i in range(2):
                    put(T - 2 + i, i)
                for i in range(2):
                    pool.wait_ge(rows_out[i], 16 * (T // 2))

        @block.vector
        def _(dve):
            v = nc.vector
            steps = Steps(dve, dve_step)
            dve.wait_ge(consts, 1)
            steps.link(v.memset(whsum[:, :], 0.0))
            dve.wait_ge(x_loaded, 16)

            STORES, SEARCH = 4, 2 * (1 + 1 + 5) + 6 + 2 * 5 + 1
            PAIR = STORES + SEARCH

            def flat(t):
                return t.rearrange("p a b -> p (a b)")

            def store_pair(u):
                for i in range(2):
                    dve.wait_ge(wh_psum, 2 * u + 2)
                    if not first(u):
                        dve.wait_ge(table0_out[i], 16 * u)
                    v.tensor_copy(stage[i][:, :], ps_wh[i]).then_inc(stage_ready, 1)
                    steps.link(v.tensor_copy(col(src, 2 * u + i), ps_wh[i][:, F + 1:F + 2]))
                    steps.link(v.tensor_tensor(whsum[:, :], whsum[:, :], ps_wh[i], ALU.add))

            def extract_pair(u):
                if first(u):
                    steps.start(1)
                else:
                    steps.start(1 - STORES + PAIR * u)
                    store_pair(u - 1)
                for i in range(2):
                    t = 2 * u + i
                    dve.nop(nofuse=True)
                    steps.link(v.bn_stats(out=bn[:, :], in_=row(x_nodes, t)), alone=True)
                    v.bn_aggr(out=mv[i][:, :], in_=bn[:, :]).then_inc(var_ready, 1)
                    dve.wait_ge(var_ready, t + 1)
                    v.tensor_scalar(hc[i][:, :], row(x_nodes, t), mv[i][:, 0:1], 0.0, ALU.subtract, ALU.max).then_inc(hc_ready, 1)
                for i in range(2):
                    t = 2 * u + i
                    dve.wait_ge(folded, t + 1)
                    v.scalar_tensor_tensor(out=words[:, :], in0=flat(ps_fold[i][:, :, :]), scalar=float(N),
                                           in1=flat(colbase[:, :, :]), op0=ALU.mult, op1=ALU.add).then_inc(worded, 1)
                    dve.wait_ge(worded, t + 1)
                    dve.nop(nofuse=True)
                    for m in range(NSEG):
                        found = v.max(out=cand[:, m, :], in_=words[:, m * SEG:(m + 1) * SEG])
                    steps.link(found, alone=True)
                    now = cand
                    for r in range(0, CAP, 8):
                        steps.link(v.max(out=most[:, i, r:r + 8], in_=flat(now[:, :, :])), alone=True)
                        if r + 8 < CAP:
                            steps.link(v.match_replace(out=flat(left[:, :, :]), in_to_replace=most[:, i, r:r + 8],
                                                       in_values=flat(now[:, :, :]), imm_value=0.0), alone=True)
                        now = left
                steps.link(v.tensor_copy(mosti[:, :, :], most[:, :, :]))
                steps.link(v.tensor_scalar(wordi[:, :, :], mosti[:, :, :], N.bit_length() - 1, None, ALU.logical_shift_right))
                steps.link(v.tensor_scalar(basei[:, :, :], mosti[:, :, :], N - 1, None, ALU.bitwise_and))
                pairs = (P, 2 * CAP, FOLD)
                merged = "p a c q -> p (a c) q"
                steps.link(v.tensor_tensor(bits[:, :, :, :].rearrange(merged), flat(wordi[:, :, :]).unsqueeze(2).broadcast_to(pairs),
                                           bitval[:, :].unsqueeze(1).broadcast_to(pairs), ALU.bitwise_and))
                steps.link(v.tensor_tensor(edge[:, :, :, :].rearrange(merged), flat(basei[:, :, :]).unsqueeze(2).broadcast_to(pairs),
                                           bitcol[:, :].unsqueeze(1).broadcast_to(pairs), ALU.add))
                whole = "p a c q -> p (a c q)"
                steps.link(v.scalar_tensor_tensor(out=edge[:, :, :, :].rearrange(whole), in0=bits[:, :, :, :].rearrange(whole),
                                                  scalar=0.0, in1=edge[:, :, :, :].rearrange(whole),
                                                  op0=ALU.is_gt, op1=ALU.mult), alone=True)
                for i in range(2):
                    now = edge
                    for r in range(0, CAP, 8):
                        steps.link(v.max(out=best[:, i, r:r + 8], in_=flat(now[:, i, :, :])), alone=True)
                        if r + 8 < CAP:
                            steps.link(v.match_replace(out=flat(rest[:, i, :, :]), in_to_replace=best[:, i, r:r + 8],
                                                       in_values=flat(now[:, i, :, :]), imm_value=0.0), alone=True)
                        now = rest
                steps.link(v.tensor_copy(top[:, bass.ds(2 * u, 2), :], best[:, :, :]))
                if first(u):
                    assert steps.at == SEARCH, steps.at
                else:
                    assert steps.at == PAIR, steps.at

            from_first(dve, T // 2, extract_pair)
            steps.start(1 - STORES + PAIR * (T // 2))
            store_pair(T // 2 - 1)
            v.memset(over1[:, :], 0.0).then_inc(whsum_ready, 1)
            dve.wait_ge(mean_psum, 1)
            steps.link(v.tensor_scalar(meanb[:, :], ps_small[:, 0:F], 1.0 / N, None, ALU.mult))
            steps.link(v.memset(whsum[:, :], 0.0))

            link = steps.link
            keyv = top[:, :, :]
            ownb = own[:, :].unsqueeze(2).broadcast_to((P, T, CAP))
            link(v.tensor_scalar(valid, keyv, float(N), None, ALU.is_ge))
            link(v.scalar_tensor_tensor(out=nbr, in0=keyv, scalar=-float(N), in1=ownb, op0=ALU.add, op1=ALU.subtract))
            link(v.tensor_tensor(nbr, nbr, valid, ALU.mult))
            link(v.tensor_tensor(rec[:, :, 0:CAP], nbr, ownb, ALU.add))
            link(v.tensor_copy(rec[:, :, OWN], own[:, :]))
            link(v.tensor_reduce(out=deg[:, :], in_=valid, axis=AX.X, op=ALU.add))
            link(v.tensor_copy(rec[:, :, DEG], deg[:, :]))
            link(v.tensor_copy(rec[:, :, SRC], src[:, :]))
            link(v.tensor_tensor(rec[:, :, MISS], total[:, :], deg[:, :], ALU.not_equal))
            link(v.memset(zeros_v, 0.0))
            link(v.memset(zeros_s[:, :], 0.0))
            link(v.tensor_tensor(is_v, deg[:, :].unsqueeze(1).broadcast_to((P, NV, T)),
                                 degval[:, :].unsqueeze(2).broadcast_to((P, NV, T)), ALU.is_equal))
            v.tensor_reduce(out=cnt[:, :], in_=is_v, axis=AX.X, op=ALU.add).then_inc(cnt_ready, 1)
            dve.wait_ge(cnt_ready, 1)
            link(v.tensor_tensor_scan(flat(run_v), flat(is_v), flat(zeros_v), 0.0, ALU.add, ALU.add))
            link(v.tensor_tensor_scan(cpre[:, :], cnt[:, :], zeros_s[:, :], 0.0, ALU.add, ALU.add))
            dve.wait_ge(cnt_summed, 1)
            link(v.tensor_tensor_scan(tpre[:, :], ps_small[:, W:W + NV], zeros_s[:, :], 0.0, ALU.add, ALU.add))
            link(v.tensor_tensor(tpre[:, :], tpre[:, :], ps_small[:, W:W + NV], ALU.subtract))
            link(v.tensor_tensor(cpre[:, :], cpre[:, :], cnt[:, :], ALU.subtract))
            link(v.tensor_tensor(base_v[:, :], tpre[:, :], ps_small[:, 0:NV], ALU.add))
            link(v.tensor_tensor(base_v[:, :], base_v[:, :], cpre[:, :], ALU.subtract))
            link(v.tensor_tensor(run_v, run_v, base_v[:, :].unsqueeze(2).broadcast_to((P, NV, T)), ALU.add))
            link(v.tensor_tensor(run_v, run_v, is_v, ALU.mult))
            link(v.tensor_reduce(out=rankv[:, :], in_=run_v.rearrange("p v t -> p t v"), axis=AX.X, op=ALU.add))
            v.tensor_scalar(rank[:, :], rankv[:, :], -1.0, None, ALU.add).then_inc(ranked, 1)

            dve.wait_ge(sorted_in, 32)
            link(v.tensor_copy(sdeg, srec[:, :, DEG]))
            link(v.tensor_copy(src[:, :], srec[:, :, SRC]))
            slotb = slot[:, :].unsqueeze(1).broadcast_to((P, T, CAP))
            sdegb = sdeg.unsqueeze(2).broadcast_to((P, T, CAP))
            link(v.tensor_tensor(pad, slotb, sdegb, ALU.is_ge))
            link(v.tensor_scalar(pad, pad, PAD, None, ALU.mult))
            link(v.tensor_tensor(once, slotb, sdegb, ALU.is_lt))
            link(v.tensor_scalar(nonempty[:, :], sdeg, 0.0, None, ALU.is_gt))
            link(v.tensor_scalar(empty[:, :], sdeg, 0.0, None, ALU.is_equal))
            link(v.tensor_tensor(over[:, :], sdeg, bound[:, :], ALU.is_gt))
            link(v.tensor_tensor(over[:, :], over[:, :], srec[:, :, MISS], ALU.max))
            v.tensor_reduce(out=over1[:, :], in_=over[:, :], axis=AX.X, op=ALU.max).then_inc(over_ready, 1)
            dve.wait_ge(over_summed, 1)
            v.tensor_scalar(flag[:, :], ps_small[0:1, 0:1], 0.0, None, ALU.is_gt).then_inc(flag_ready, 1)

            dve.wait_ge(flag_ready, 1)
            after_rank = steps.total()
            dense = dve.value_load(flag[0:1, 0:1], min_val=0, max_val=1)
            with dve.If(dense > 0):
                done = after_rank
                dve.wait_ge(d_x_in, 16)
                for n, (kind, slope, elu) in enumerate(LAYERS):
                    g = gat_no.get(n)
                    PREP = 1
                    with dve.Fori(0, T) as t:
                        steps.start(done + PREP * t)
                        steps.link(v.bn_stats(out=bn[:, :], in_=row(X, t)), alone=True)
                        v.bn_aggr(out=mv[0][:, :], in_=bn[:, :]).then_inc(d_var, 1)
                        dve.wait_ge(d_rstd, n * T + t + 1)
                        v.tensor_scalar(hc[0][:, :], row(X, t), mv[0][:, 0:1], 0.0, ALU.subtract, ALU.max).then_inc(d_hc, 1)
                        if kind == GAT:
                            dve.wait_ge(d_whp, g * T + t + 1)
                            v.tensor_copy(row(H, t), ps_wh[0]).then_inc(d_wh, 1)
                        else:
                            dve.wait_ge(d_h, n * T + t + 1)
                            v.tensor_copy(row(H, t)[:, 0:F], h[0][:, :]).then_inc(d_wh, 1)
                        dve.wait_ge(d_wh, n * T + t + 1)
                        dve.nop(nofuse=True)
                        assert steps.at == PREP
                    done = done + PREP * T
                    if kind == GAT:
                        dve.wait_ge(d_dst_in, 16 * (g + 1))
                    dve.sem_inc(d_adj_free, 1)

                    ROWS = {0: 9, 1: 9, 2: 2, 3: 9}[n]
                    with dve.Fori(0, T) as t:
                        steps.start(done + ROWS * t)
                        dve.wait_ge(d_adj_in, 16 * (n * T + t + 1))
                        if kind == GAT:
                            link = steps.link
                            link(v.tensor_scalar(d_z, d_dst, row(H, t)[:, F + 1:F + 2], None, ALU.add))
                            link(v.scalar_tensor_tensor(out=d_z, in0=d_z, scalar=slope, in1=d_z, op0=ALU.mult, op1=ALU.max))
                            link(v.scalar_tensor_tensor(out=d_t, in0=d_adj[:, :], scalar=0.0, in1=d_z,
                                                        op0=ALU.is_gt, op1=ALU.mult))
                            v.tensor_scalar(d_z, d_adj[:, :], 0.0, NEG_INF[n], ALU.is_le, ALU.mult).then_inc(d_adj_free, 1)
                            dve.wait_ge(d_adj_free, n * (T + 1) + t + 2)
                            link(v.tensor_tensor(d_z, d_z, d_t, ALU.add))
                            link(v.tensor_reduce(out=nmax[1][:, :], in_=d_z, axis=AX.X, op=ALU.max))
                            v.tensor_scalar(nmax[0][:, :], nmax[1][:, :], -1.0, None, ALU.mult).then_inc(d_z_ready, 1)
                            dve.wait_ge(d_p_ready, g * T + t + 1)
                        else:
                            v.tensor_scalar(d_z, d_adj[:, :], 1.0, None, ALU.is_equal).then_inc(d_adj_free, 1)
                            dve.wait_ge(d_adj_free, n * (T + 1) + t + 2)
                            dve.sem_inc(d_z_ready, 1)
                        steps.link(v.memset(acc[0][:, :], 0.0), alone=True)
                        with dve.Fori(0, T // 4) as gr:
                            dve.wait_ge(d_op, (n * T + t) * (T // 4) + gr + 1)
                            v.tensor_tensor(acc[0][:, :], acc[0][:, :], ps_o, ALU.add).then_inc(d_acc, 1)
                            dve.wait_ge(d_acc, (n * T + t) * (T // 4) + gr + 1)
                            dve.nop(nofuse=True)
                        if kind == SUM:
                            steps.link(v.tensor_tensor(acc[0][:, :], acc[0][:, :], row(H, t)[:, 0:F], ALU.add))
                            v.tensor_tensor(row(X, t), row(X, t), acc[0][:, :], ALU.add).then_inc(d_done, 1)
                        else:
                            steps.link(v.reciprocal(rinv[:, :], rsum[0][:, :]))
                            steps.link(v.tensor_scalar(hp[0][:, :], acc[0][:, :], rinv[:, 0:1], None, ALU.mult))
                            if elu:
                                v.tensor_scalar(low[0][:, :], hp[0][:, :], 0.0, None, ALU.min).then_inc(d_low, 1)
                                dve.wait_ge(d_ex, g * T + t + 1)
                                steps.link(v.scalar_tensor_tensor(out=tmp[:, :], in0=hp[0][:, :], scalar=0.0, in1=ex[0][:, :],
                                                                  op0=ALU.max, op1=ALU.add))
                                v.scalar_tensor_tensor(out=row(X, t), in0=tmp[:, :], scalar=-1.0, in1=row(X, t),
                                                       op0=ALU.add, op1=ALU.add).then_inc(d_done, 1)
                            else:
                                steps.link(v.tensor_tensor(tmp[:, :], hp[0][:, :], biasb[:, :], ALU.add))
                                v.tensor_tensor(row(X, t), row(X, t), tmp[:, :], ALU.add).then_inc(d_done, 1)
                        dve.wait_ge(d_done, n * T + t + 1)
                        dve.nop(nofuse=True)
                        assert steps.at == ROWS, (n, steps.at)
                    done = done + ROWS * T
            with dve.Else():
                done = after_rank
                for q, (kind, slope, elu) in enumerate(LAYERS):
                    last = q == 3
                    SCORES = {0: 3, 1: 2, 2: 0, 3: 2}[q]
                    ROWSUM = 5 if kind == GAT else 1
                    UPDATE = 1 if last else 3
                    STORE = 0 if last else (1 if q == 1 else 2)
                    PER = SCORES + ROWSUM + UPDATE + STORE

                    def scores(q, k, i, slots):
                        g = gathered[i]
                        if q == 0:
                            steps.link(v.tensor_copy(row(srec, k)[:, 0:slots], g[:, 0:slots, RANK]))
                        steps.link(v.tensor_scalar(score[i][:, 0:slots], g[:, 0:slots, F], -1.0,
                                                   col(src, k), ALU.mult, ALU.subtract))
                        steps.link(v.scalar_tensor_tensor(out=score[i][:, 0:slots], in0=score[i][:, 0:slots], scalar=slope,
                                                          in1=score[i][:, 0:slots], op0=ALU.mult, op1=ALU.min), alone=True)
                        v.tensor_tensor_reduce(out=score[i][:, 0:slots], in0=score[i][:, 0:slots],
                                               in1=pads[i][:, 0:slots], scale=1.0, scalar=BIG, op0=ALU.add,
                                               op1=ALU.min, accum_out=nmax[i][:, :]).then_inc(score_ready, 1)

                    def rowsum(q, k, i, slots):
                        g = gathered[i]
                        if kind == GAT:
                            dve.wait_ge(prob_ready, T * gat_no[q] + k + 1)
                            weight = prob[i][:, 0:slots]
                        else:
                            weight = row(once, k)[:, 0:slots]
                        v.tensor_tensor(prod[:, 0:slots, :], g[:, 0:slots, 0:F],
                                        weight.unsqueeze(2).broadcast_to((P, slots, F)), ALU.mult).then_inc(gather_free, 1)
                        dve.wait_ge(gather_free, T * q + k + 1)
                        steps.link(v.tensor_reduce(out=acc[i][:, :], in_=prod[:, 0:slots, :].rearrange("p b f -> p f b"),
                                                   axis=AX.X, op=ALU.add))
                        if kind == GAT:
                            steps.link(v.reciprocal(rinv[:, :], rsum[i][:, :]))
                            steps.link(v.tensor_tensor(rinv[:, :], rinv[:, :], col(nonempty, k), ALU.mult))
                            steps.link(v.tensor_scalar(fill[:, :], meanb[:, :], col(empty, k), None, ALU.mult))
                            steps.link(v.scalar_tensor_tensor(out=hp[i][:, :], in0=acc[i][:, :], scalar=rinv[:, 0:1],
                                                              in1=fill[:, :], op0=ALU.mult, op1=ALU.add))
                            if elu:
                                v.tensor_scalar(low[i][:, :], hp[i][:, :], 0.0, None, ALU.min).then_inc(low_ready, 1)

                    def update(q, k, i):
                        if kind == SUM:
                            steps.link(v.tensor_tensor(tmp[:, :], acc[i][:, :], row(H, k)[:, 0:F], ALU.add))
                            steps.link(v.tensor_tensor(row(X, k), row(X, k), tmp[:, :], ALU.add))
                        elif elu:
                            dve.wait_ge(ex_ready, T * gat_no[q] + k + 1)
                            steps.link(v.scalar_tensor_tensor(out=tmp[:, :], in0=hp[i][:, :], scalar=0.0, in1=ex[i][:, :],
                                                              op0=ALU.max, op1=ALU.add))
                            steps.link(v.scalar_tensor_tensor(out=row(X, k), in0=tmp[:, :], scalar=-1.0, in1=row(X, k),
                                                              op0=ALU.add, op1=ALU.add))
                        else:
                            steps.link(v.tensor_tensor(tmp[:, :], hp[i][:, :], biasb[:, :], ALU.add))
                            if not (isinstance(k, int) and k < 2):
                                dve.wait_ge(rows_out[i], 8 * (k - i))
                            if isinstance(k, int) and k < 2:
                                dve.wait_ge(table_out[i], 16 * (T // 2 * q))
                            v.tensor_tensor(stage[i][:, 0:F], row(X, k), tmp[:, :], ALU.add).then_inc(stage_ready, 1)
                        if not last:
                            dve.nop(nofuse=True)
                            steps.link(v.bn_stats(out=bn[:, :], in_=row(X, k)), alone=True)
                            v.bn_aggr(out=mv[i][:, :], in_=bn[:, :]).then_inc(var_ready, 1)
                            dve.wait_ge(var_ready, after + T * q + k + 1)
                            v.tensor_scalar(hc[i][:, :], row(X, k), mv[i][:, 0:1], 0.0, ALU.subtract, ALU.max).then_inc(hc_ready, 1)

                    def store(q, k, i):
                        if q or not isinstance(k, int) or k >= 2:
                            dve.wait_ge(table_out[i], 16 * (T // 2 * q) + 8 * (k - i))
                        if q == 1:
                            dve.wait_ge(h_ready, after + T * q + k + 1)
                            v.tensor_copy(stage[i][:, 0:F], h[i][:, :]).then_inc(stage_ready, 1)
                            steps.link(v.tensor_copy(row(H, k)[:, 0:F], h[i][:, :]))
                        else:
                            dve.wait_ge(wh_psum, after + T * (q // 2) + k + 1)
                            v.tensor_copy(stage[i][:, :], ps_wh[i]).then_inc(stage_ready, 1)
                            steps.link(v.tensor_copy(col(src, k), ps_wh[i][:, F + 1:F + 2]))
                            steps.link(v.tensor_tensor(whsum[:, :], whsum[:, :], ps_wh[i], ALU.add))

                    def tile(k, i, slots, upto):
                        dve.wait_ge(gather_in[i], 16 * upto)
                        if kind == GAT:
                            scores(q, k, i, slots)
                        if not (isinstance(k, int) and k == 0):
                            update(q, k - 1, 1 - i)
                        rowsum(q, k, i, slots)
                        if not (isinstance(k, int) and k == 0) and not last:
                            store(q, k - 1, 1 - i)

                    def pair(u, slots, upto):
                        for i in range(2):
                            k = 2 * u + i
                            if isinstance(k, int) and k == 0:
                                steps.start(done)
                                tile(k, i, slots[i], upto[i])
                                assert steps.at == PER - UPDATE - STORE, (q, steps.at)
                            else:
                                steps.start(done - UPDATE - STORE + PER * k)
                                tile(k, i, slots[i], upto[i])
                                assert steps.at == PER, (q, steps.at)

                    each_pair(dve, q, pair)
                    steps.start(done - UPDATE - STORE + PER * T)
                    update(q, T - 1, 1)
                    if not last:
                        store(q, T - 1, 1)
                    assert steps.at == UPDATE + STORE
                    done = done + PER * T
                    if q in weights:
                        dve.sem_inc(whsum_ready, 1)
                        dve.wait_ge(mean_psum, weights[q] + 1)
                        steps.start(done)
                        steps.link(v.tensor_scalar(meanb[:, :], ps_small[:, 0:F], 1.0 / N, None, ALU.mult))
                        steps.link(v.memset(whsum[:, :], 0.0))
                        done = done + 2

        @block.scalar
        def _(act):
            s = nc.scalar
            act.preload_act_table_set("natural_log_exp_and_others")
            for i in range(3):
                act.wait_ge(w_t, i + 1)
                s.copy(wT[i][:, :], ps_hT[0][:, 0:F]).then_inc(w_tc, 1)
            for i in range(3):
                act.wait_ge(w_a, i + 1)
                s.copy(wcat[i][:, F:W], ps_hT[1][:, 0:2]).then_inc(w_ready, 1)

            def normalise(n, k, i, p=None):
                act.wait_ge(var_ready, n + k + 1)
                s.activation(lnv[i][:, :], mv[i][:, 1:2], ACT.Ln, bias=epsc[:, 0:1]).then_inc(ln_ready, 1)
                act.wait_ge(ln_ready, n + k + 1)
                s.activation(rstd[i][:, :], lnv[i][:, :], ACT.Exp, scale=-0.5).then_inc(rstd_ready, 1)
                act.wait_ge(rstd_ready, n + k + 1)
                act.wait_ge(hc_ready, n + k + 1)
                s.activation(h[i][:, :], hc[i][:, :], ACT.Copy, scale=rstd[i][:, 0:1]).then_inc(h_ready, 1)
                if p is not None:
                    act.wait_ge(hT_psum, p + k + 1)
                    s.copy(hT[i][:, :], ps_hT[i]).then_inc(hT_ready, 1)

            def narrow_pair(t, j, turn):
                for i in range(2):
                    act.wait_ge(adj_loaded[(j + i) % 3], 16 * turn[i])
                    if not (isinstance(t, int) and t == 0):
                        act.wait_ge(folded, t + i - 1)
                    s.activation(adj_bf[:, i, :], adj_in[(j + i) % 3][:, :], ACT.Relu,
                                 accum_out=col(total, t + i)).then_inc(narrowed, 1)
                for i in range(2):
                    normalise(0, t + i, i, 0)

            def six(v6):
                for j in range(0, 6, 2):
                    narrow_pair(6 * v6 + j, j, [2 * v6 + (j + i) // 3 + 1 for i in range(2)])

            from_first(act, (T - 4) // 6, six)
            for t in (T - 4, T - 2):
                narrow_pair(t, t % 3, [(t + i) // 3 + 1 for i in range(2)])

            act.wait_ge(ranked, 1)
            def stage_records(t4):
                for i in range(4):
                    t = 4 * t4 + i
                    if not first(t4):
                        act.wait_ge(scattered[i], 16 * t4)
                    s.copy(recs[i][:, 0:FEAT], row(rec, t)).then_inc(rec_staged, 1)
                    s.copy(recs[i][:, FEAT:REC], row(x_nodes, t)).then_inc(rec_staged, 1)
                    s.copy(places[i][:, :], col(rank, t)).then_inc(rec_staged, 1)

            from_first(act, T // 4, stage_records)

            act.wait_ge(flag_ready, 1)
            dense = act.value_load(flag[0:1, 0:1], min_val=0, max_val=1)

            with act.If(dense > 0):
                for n, (kind, _slope, elu) in enumerate(LAYERS):
                    g = gat_no.get(n)
                    with act.Fori(0, T) as t:
                        act.wait_ge(d_var, n * T + t + 1)
                        s.activation(lnv[0][:, :], mv[0][:, 1:2], ACT.Ln, bias=epsc[:, 0:1]).then_inc(d_ln, 1)
                        act.wait_ge(d_ln, n * T + t + 1)
                        s.activation(rstd[0][:, :], lnv[0][:, :], ACT.Exp, scale=-0.5).then_inc(d_rstd, 1)
                        act.wait_ge(d_rstd, n * T + t + 1)
                        act.wait_ge(d_hc, n * T + t + 1)
                        s.activation(h[0][:, :], hc[0][:, :], ACT.Copy, scale=rstd[0][:, 0:1]).then_inc(d_h, 1)
                        if kind == GAT:
                            act.wait_ge(d_hTp, g * T + t + 1)
                            s.copy(hT[0][:, :], ps_hT[0]).then_inc(d_hT, 1)
                    with act.Fori(0, T) as t:
                        if kind == GAT:
                            act.wait_ge(d_z_ready, n * T + t + 1)
                            s.activation(d_z, d_z, ACT.Exp, bias=nmax[0][:, 0:1], accum_out=rsum[0][:, 0:1]).then_inc(d_p_ready, 1)
                            act.wait_ge(d_p_ready, g * T + t + 1)
                        else:
                            act.wait_ge(d_z_ready, n * T + t + 1)
                        with act.Fori(0, T // 4) as gr:
                            s.copy(zs, d_z[:, bass.ds(gr * (4 * P), 4 * P)]).then_inc(d_zs, 1)
                            act.wait_ge(d_zTp, (n * T + t) * (T // 4) + gr + 1)
                            s.copy(zT, ps_z).then_inc(d_zT, 1)
                            act.wait_ge(d_acc, (n * T + t) * (T // 4) + gr + 1)
                        if elu:
                            act.wait_ge(d_low, g * T + t + 1)
                            s.activation(ex[0][:, :], low[0][:, :], ACT.Exp).then_inc(d_ex, 1)
            with act.Else():
                act.wait_ge(sorted_in, 32)

                def stage_ids(k, i):
                    s.copy(pads[i][:, :], row(pad, k)).then_inc(ids_ready, 1)
                    s.copy(ids[i][:, :], row(srec, k)[:, 0:CAP + 1]).then_inc(ids_ready, 1)

                stage_ids(0, 0)
                stage_ids(1, 1)
                for q, (kind, _slope, elu) in enumerate(LAYERS):
                    last = q == 3
                    proj = None if q == 1 else after + T * (q // 2)

                    def pair(u, slots, upto, q=q, kind=kind, elu=elu, last=last, proj=proj):
                        for i in range(2):
                            k = 2 * u + i
                            start = isinstance(u, int) and u == 0
                            if kind == GAT:
                                act.wait_ge(score_ready, T * gat_no[q] + k + 1)
                                s.activation(prob[i][:, 0:slots[i]], score[i][:, 0:slots[i]], ACT.Exp, bias=nmax[i][:, 0:1],
                                             scale=-1.0, accum_out=rsum[i][:, 0:1]).then_inc(prob_ready, 1)
                            if not last and not (start and i == 0):
                                normalise(after + T * q, k - 1, 1 - i, proj)
                            if elu:
                                act.wait_ge(low_ready, T * gat_no[q] + k + 1)
                                s.activation(ex[i][:, :], low[i][:, :], ACT.Exp).then_inc(ex_ready, 1)
                            if not (last and isinstance(u, int) and u == T // 2 - 1):
                                act.wait_ge(gather_in[i], 16 * upto[i])
                                nxt = i if isinstance(u, int) and u == T // 2 - 1 else k + 2
                                stage_ids(nxt, i)
                            if last:
                                if not start:
                                    act.wait_ge(rows_out[i], 16 * u)
                                s.copy(owns[i][:, :], row(srec, k)[:, OWN:OWN + 1]).then_inc(owns_ready, 1)

                    each_pair(act, q, pair)
                    if not last:
                        normalise(after + T * q, T - 1, 1, proj)

        @block.tensor
        def _(pe):
            mm = nc.tensor.matmul
            pe.wait_ge(consts, 1)
            pe.wait_ge(params, 16 * 10)
            for i in range(3):
                if i:
                    pe.wait_ge(w_tc, i)
                nc.tensor.transpose(ps_hT[0][:, 0:F], wcat[i][:, 0:F], ident[0:F, 0:F]).then_inc(w_t, 1)
            for i in range(3):
                pe.wait_ge(w_tc, i + 1)
                if i:
                    pe.wait_ge(w_ready, i)
                mm(ps_hT[1][:, 0:2], wT[i][:, :], acol[i][:, :], start=True, stop=True).then_inc(w_a, 1)
            pe.wait_ge(w_ready, 3)

            def project(n, p, w, k, i):
                pe.wait_ge(h_ready, n + k + 1)
                pe.nop(nofuse=True)
                nc.tensor.transpose(ps_hT[i], h[i][:, :], ident[:, :]).then_inc(hT_psum, 1)
                pe.wait_ge(hT_ready, p + k + 1)
                mm(ps_wh[i], hT[i][:, :], wcat[w][:, :], start=True, stop=True).then_inc(wh_psum, 1)

            def fold_pair(u):
                for i in range(2):
                    t = 2 * u + i
                    pe.wait_ge(narrowed, t + 1)
                    if not first(u):
                        pe.wait_ge(worded, t - 1)
                    for half in range(2):
                        for q in range(FOLD):
                            c = half * (N // 2) + q * FC
                            done = mm(ps_fold[i][:, half, :], diag[:, q, :], adj_bf[:, i, c:c + FC],
                                      start=q == 0, stop=q == FOLD - 1)
                    done.then_inc(folded, 1)
                for i in range(2):
                    project(0, 0, 0, 2 * u + i, i)

            from_first(pe, T // 2, fold_pair)
            pe.wait_ge(whsum_ready, 1)
            mm(ps_small[:, 0:F], ones[:, :], whsum[:, 0:F], start=True, stop=True).then_inc(mean_psum, 1)
            pe.wait_ge(cnt_ready, 1)
            mm(ps_small[:, 0:NV], lower[:, :], cnt[:, :], start=True, stop=True)
            mm(ps_small[:, W:W + NV], ones[:, :], cnt[:, :], start=True, stop=True).then_inc(cnt_summed, 1)
            pe.wait_ge(over_ready, 1)
            mm(ps_small[:, 0:1], ones[:, :], over1[:, :], start=True, stop=True).then_inc(over_summed, 1)

            pe.wait_ge(flag_ready, 1)
            dense = pe.value_load(flag[0:1, 0:1], min_val=0, max_val=1)
            with pe.If(dense > 0):
                for n, (kind, _slope, _elu) in enumerate(LAYERS):
                    g = gat_no.get(n)
                    if kind == GAT:
                        with pe.Fori(0, T) as t:
                            pe.wait_ge(d_h, n * T + t + 1)
                            pe.nop(nofuse=True)
                            nc.tensor.transpose(ps_hT[0], h[0][:, :], ident[:, :]).then_inc(d_hTp, 1)
                            pe.wait_ge(d_hT, g * T + t + 1)
                            mm(ps_wh[0], hT[0][:, :], wcat[g][:, :], start=True, stop=True).then_inc(d_whp, 1)
                    with pe.Fori(0, T) as t:
                        with pe.Fori(0, T // 4) as gr:
                            now = (n * T + t) * (T // 4) + gr + 1
                            pe.wait_ge(d_zs, now)
                            for c in range(4):
                                tr = nc.tensor.transpose(ps_z[:, c * P:(c + 1) * P], zs[:, c * P:(c + 1) * P], ident[:, :])
                            tr.then_inc(d_zTp, 1)
                            pe.wait_ge(d_zT, now)
                            for c in range(4):
                                last = mm(ps_o, zT[:, c * P:(c + 1) * P],
                                          H[:, bass.ds(gr * 4 + c, 1), 0:F].rearrange("p a f -> p (a f)"),
                                          start=c == 0, stop=c == 3)
                            last.then_inc(d_op, 1)
            with pe.Else():
                for q, w in weights.items():
                    with pe.Fori(0, T // 2) as u:
                        for i in range(2):
                            project(after + T * q, after + T * (q // 2), w, 2 * u + i, i)
                    pe.wait_ge(whsum_ready, w + 1)
                    mm(ps_small[:, 0:F], ones[:, :], whsum[:, 0:F], start=True, stop=True).then_inc(mean_psum, 1)


_INS = ["x", "adj", "L0_gnn_W", "L0_gnn_a", "L1_gnn_W", "L1_gnn_a", "L3_gnn_weight_w", "L3_gnn_weight_a", "L3_gnn_bias"]


def kernel(**inputs):
    import numpy as np
    import concourse.bacc as bacc
    from concourse.bass_utils import run_bass_kernel_spmd

    nc = bacc.Bacc("TRN2", target_bir_lowering=False, num_devices=1)
    arrays, args = {}, []
    for name in _INS:
        a = np.ascontiguousarray(inputs[name])
        arrays[f"in_{name}"] = a
        args.append(nc.dram_tensor(f"in_{name}", a.shape, mybir.dt.from_np(a.dtype), kind="ExternalInput").ap())
    out = nc.dram_tensor("out_x", (N, F), f32, kind="ExternalOutput").ap()
    build(nc, *args, out)
    r = run_bass_kernel_spmd(nc, [arrays], core_ids=[0])
    return r.results[0]["out_x"]
```

```python
from contextlib import ExitStack
from math import exp, factorial

import concourse.bass as bass
from concourse import mybir

f32 = mybir.dt.float32
i32 = mybir.dt.int32
bf16 = mybir.dt.bfloat16
ALU = mybir.AluOpType
ACT = mybir.ActivationFunctionType
AX = mybir.AxisListType

N = 8192
F = 64
P = 128
T = N // P
FOLD = 8
FC = 512
WORDS = N // FOLD
SEG = 64
NSEG = WORDS // SEG
CAP = 24
W = F + 2
RANK = F + 1
EARLY = 8
GROUP = 4
OWN, DEG, SRC, LEAST, SUM1, PART = CAP, CAP + 1, CAP + 2, CAP + 3, CAP + 4, CAP + 5
FEAT = PART + F
REC = FEAT + F
COLS = PART - CAP
EPS = 1e-5
PAD = 1e38
BIG = 3e38
EDGE_RATE = 1.0 / 1024

GAT, SUM = "gat", "sum"
LAYERS = [(GAT, 0.2, True), (GAT, 0.2, True), (SUM, None, False), (GAT, 0.01, False)]
NEG_INF = [-9e15, -9e15, None, -1e9]


def degree_bounds():
    mean = N * EDGE_RATE
    pmf = [exp(-mean) * mean ** k / factorial(k) for k in range(60)]
    out = [CAP]
    for first in range(P, N, P):
        for b in range(1, CAP + 1):
            above = N * sum(pmf[b + 1:])
            if above + 4 * above ** 0.5 + (3 if above < 9 else 0) <= first or b == CAP:
                out.append(b)
                break
    return out


BOUNDS = degree_bounds()
LATE = [max(b - EARLY, 0) for b in BOUNDS]


def slots_of(bounds):
    return [sum(bounds[i::2]) for i in range(2)]


def pair_runs(bounds):
    runs, before = [], (0, 0)
    for u in range(T // 2):
        b = tuple(bounds[2 * u:2 * u + 2])
        if runs and u not in (1, T // 2 - 1) and runs[-1][2] == b:
            runs[-1][1] = u + 1
        else:
            runs.append([u, u + 1, b, before])
        before = (before[0] + b[0], before[1] + b[1])
    return [tuple(r) for r in runs]


RUNS = [pair_runs(LATE if q == 0 else BOUNDS) for q in range(4)]
BEFORE = [[0, 0]] + [[slots_of(LATE)[i] + q * slots_of(BOUNDS)[i] for i in range(2)] for q in range(3)]


class Steps:

    def __init__(self, eng, sem):
        self.eng, self.sem, self.base, self.at = eng, sem, 0, 0

    def mark(self, ins):
        self.at += 1
        ins.then_inc(self.sem, 1)
        return self.at

    def after(self, n, alone=False):
        self.eng.wait_ge(self.sem, self.base + n)
        if alone:
            self.eng.nop(nofuse=True)

    def link(self, ins, alone=False):
        self.after(self.mark(ins), alone)

    def total(self):
        return self.base + self.at

    def start(self, base):
        self.base, self.at = base, 0


def build(nc, x, adj, w0, a0, w1, a1, w3, a3, bias3, out):
    ctx = ExitStack()
    with ctx:
        def sb(name, shape, dt=f32):
            return ctx.enter_context(nc.sbuf_tensor(name, shape, dt))

        def ps(name, shape):
            return ctx.enter_context(nc.psum_tensor(name, shape, f32))

        def sem(name):
            return ctx.enter_context(nc.semaphore(name))

        records_d = nc.dram_tensor("records_d", [N, REC], f32).ap()
        width = [F + 1, F + 2, F, F + 1]
        tables = [nc.dram_tensor(f"table{q}", [N, width[q]], f32).ap() for q in range(4)]
        dst_d = [nc.dram_tensor(f"dst{i}", [1, N], f32).ap() for i in range(4)]

        adj_in = [sb(f"adj_in{i}", [P, N], i32) for i in range(3)]
        adj_bf = sb("adj_bf", [P, 2, N], bf16)
        X = sb("X", [P, T, F])
        H = sb("H", [P, T, W])
        top = sb("top", [P, T, CAP])
        words = sb("words", [P, WORDS])
        colbase = sb("colbase", [P, 2, FC])
        cand = sb("cand", [P, 2, NSEG * 8])
        left = sb("left", [P, 2, NSEG * 8])
        most = sb("most", [P, 2, CAP])
        mosti = sb("mosti", [P, 2, CAP], i32)
        wordi = sb("wordi", [P, 2, CAP], i32)
        basei = sb("basei", [P, 2, CAP], i32)
        bitval = sb("bitval", [P, FOLD], i32)
        bitcol = sb("bitcol", [P, FOLD])
        bits = sb("bits", [P, 2, CAP, FOLD], i32)
        edge = sb("edge", [P, 2, CAP, FOLD])
        rest = sb("rest", [P, 2, CAP, FOLD])
        best = sb("best", [P, 2, CAP])
        valid = sb("valid", [P, 2, CAP])
        nbr = sb("nbr", [P, 2, CAP])
        total = sb("total", [P, T])
        diag = sb("diag", [P, FOLD, P], bf16)

        def carve(region, sizes):
            views, at = [], 0
            for shape in sizes:
                n = 1
                for m in shape:
                    n *= m
                v = region[:, at:at + n].bitcast(f32)
                if len(shape) == 2:
                    v = v.rearrange("p (a b) -> p a b", a=shape[0])
                views.append(v)
                at += n
            assert at <= N
            return views

        NV = CAP + 1
        x_nodes = H[:, :, 0:F]
        is_v, run_v = carve(adj_in[0][:, :], [(NV, T), (NV, T)])
        g0, g1, prod = carve(adj_in[1][:, :], [(CAP, W), (CAP, W), (CAP, F)])
        gathered = [g0, g1]
        pad, once, sdeg, srec = carve(adj_in[2][:, :], [(T, CAP), (T, CAP), (T,), (T, PART)])
        d_adj = adj_in[0]
        d_z = adj_in[1][:, :].bitcast(f32)
        d_t = adj_in[2][:, :].bitcast(f32)
        zs, zT = words[:, 0:4 * P], words[:, 4 * P:8 * P]
        d_dst = adj_bf[:, :, :].rearrange("p a n -> p (a n)").bitcast(f32)

        ident = sb("ident", [P, P])
        ones = sb("ones", [P, P])
        lower = sb("lower", [P, P])
        nodes = sb("nodes", [P, COLS, T])
        own, deg, node_src, least, sum1 = (nodes[:, c, :] for c in range(COLS))
        dst = sb("dst", [P, T])
        x_mean = sb("x_mean", [P, T])
        x_var = sb("x_var", [P, T])
        x_rstd = sb("x_rstd", [P, T])
        h4 = [b[:, :, :, :].rearrange("p a c q -> p (a c q)")[:, 0:GROUP * F] for b in (edge, rest)]
        hT4 = [words[0:F, i * GROUP * P:(i + 1) * GROUP * P] for i in range(2)]
        x_square = adj_bf[:, 0, :].bitcast(f32).rearrange("p (t f) -> p t f", f=F)
        early = [sb(f"early{j}", [P, 2 * EARLY, F + 1]) for j in range(2)]
        early_ids = [sb(f"early_ids{j}", [P, 2, EARLY], i32) for j in range(2)]
        early_pad = [sb(f"early_pad{j}", [P, 2, EARLY]) for j in range(2)]
        early_score = sb("early_score", [P, 2, EARLY])
        early_prob = sb("early_prob", [P, 2, EARLY])
        early_sum = sb("early_sum", [P, 2])
        early_prod = words[:, 0:2 * EARLY * F].rearrange("p (a f) -> p a f", f=F)
        slot = sb("slot", [P, CAP])
        degval = sb("degval", [P, NV])
        limit = sb("limit", [P, NV])
        epsc = sb("epsc", [P, 1])
        wcat = [sb(f"wcat{i}", [F, W]) for i in range(3)]
        wT = [sb(f"wT{i}", [F, F]) for i in range(3)]
        acol = [sb(f"acol{i}", [F, 2]) for i in range(3)]
        biasb = sb("biasb", [P, F])
        nonempty = sb("nonempty", [P, T])
        empty = sb("empty", [P, T])
        cnt = sb("cnt", [P, NV])
        cpre = sb("cpre", [P, NV])
        tpre = sb("tpre", [P, NV])
        base_v = sb("base_v", [P, NV])
        zeros_s = sb("zeros_s", [P, NV])
        rank = sb("rank", [P, T])
        rankv = sb("rankv", [P, T])
        recs = [sb(f"recs{i}", [P, REC]) for i in range(4)]
        places = [sb(f"places{i}", [P, 1], i32) for i in range(4)]
        over = sb("over", [P, T])
        over_v = sb("over_v", [P, NV])
        over1 = sb("over1", [P, 2])
        flag = sb("flag", [1, 1], i32)
        ids = [sb(f"ids{i}", [P, CAP], i32) for i in range(2)]
        pads = [sb(f"pads{i}", [P, CAP]) for i in range(2)]
        owns = [sb(f"owns{i}", [P, 1], i32) for i in range(2)]
        src = sb("src", [P, T])
        score = [sb(f"score{i}", [P, CAP]) for i in range(2)]
        prob = [sb(f"prob{i}", [P, CAP]) for i in range(2)]
        nmax = [sb(f"nmax{i}", [P, 1]) for i in range(2)]
        rsum = [sb(f"rsum{i}", [P, 1]) for i in range(2)]
        rtot = sb("rtot", [P, 1])
        rinv = sb("rinv", [P, 1])
        fill = sb("fill", [P, F])
        tmp = sb("tmp", [P, F])
        bn = sb("bn", [P, 6])
        mv = [sb(f"mv{i}", [P, 2]) for i in range(2)]
        lnv = [sb(f"lnv{i}", [P, 1]) for i in range(2)]
        rstd = [sb(f"rstd{i}", [P, 1]) for i in range(2)]
        reused = [e[:, :, :].rearrange("p a c -> p (a c)") for e in early]
        acc, hp, low, ex, hc = ([reused[1][:, (2 * c + i) * F:(2 * c + i + 1) * F] for i in range(2)] for c in range(5))
        hT = [reused[0][0:F, i * P:(i + 1) * P] for i in range(2)]
        h = [reused[0][:, 2 * P + i * F:2 * P + (i + 1) * F] for i in range(2)]
        stage = [sb(f"stage{i}", [P, W]) for i in range(2)]
        whsum = sb("whsum", [P, W])
        meanb = sb("meanb", [P, F])

        ps_hT_b = [ps(f"ps_hT_b{i}", [F, 4 * P]) for i in range(2)]
        ps_hT = [b[:, 0:P] for b in ps_hT_b]
        ps_small_b = ps("ps_small_b", [P, 4 * P])
        ps_small = ps_small_b[:, 0:2 * W]
        ps_fold = [ps(f"ps_fold{i}", [P, 2, FC]) for i in range(2)]
        ps_wh = [ps_fold[i][:, 1, 0:W] for i in range(2)]
        ps_z = ps_fold[0][:, 0, :]
        ps_o = ps_fold[1][:, 0, 0:F]

        x_loaded = sem("x_loaded")
        adj_loaded = [sem(f"adj_loaded{i}") for i in range(3)]
        narrowed = sem("narrowed")
        folded = sem("folded")
        worded = sem("worded")
        x_centred = sem("x_centred")
        x_squared = sem("x_squared")
        x_summed = sem("x_summed")
        x_scaled = sem("x_scaled")
        h4_ready = sem("h4_ready")
        hT4_psum = sem("hT4_psum")
        hT4_ready = sem("hT4_ready")
        wh4_psum = sem("wh4_psum")
        wh4_taken = sem("wh4_taken")
        table0_out = sem("table0_out")
        listed = sem("listed")
        early_in = [sem(f"early_in{j}") for j in range(2)]
        early_scored = sem("early_scored")
        early_weighted = sem("early_weighted")
        early_free = sem("early_free")
        early_done = sem("early_done")
        rec_staged = sem("rec_staged")
        consts = sem("consts")
        params = sem("params")
        pool_step = sem("pool_step")
        dve_step = sem("dve_step")
        w_t = sem("w_t")
        w_tc = sem("w_tc")
        w_a = sem("w_a")
        w_ready = sem("w_ready")
        cnt_ready = sem("cnt_ready")
        cnt_summed = sem("cnt_summed")
        ranked = sem("ranked")
        scattered = [sem(f"scattered{i}") for i in range(4)]
        first_in = sem("first_in")
        sorted_in = sem("sorted_in")
        over_ready = sem("over_ready")
        over_summed = sem("over_summed")
        flag_ready = sem("flag_ready")
        masks_ready = sem("masks_ready")
        ids_ready = sem("ids_ready")
        pads_ready = sem("pads_ready")
        owns_ready = sem("owns_ready")
        gather_in = [sem(f"gather_in{i}") for i in range(2)]
        gather_free = sem("gather_free")
        table_out = [sem(f"table_out{i}") for i in range(2)]
        rows_out = [sem(f"rows_out{i}") for i in range(2)]
        stage_ready = sem("stage_ready")
        score_ready = sem("score_ready")
        prob_ready = sem("prob_ready")
        low_ready = sem("low_ready")
        ex_ready = sem("ex_ready")
        var_ready = sem("var_ready")
        ln_ready = sem("ln_ready")
        rstd_ready = sem("rstd_ready")
        hc_ready = sem("hc_ready")
        h_ready = sem("h_ready")
        hT_psum = sem("hT_psum")
        hT_ready = sem("hT_ready")
        wh_psum = sem("wh_psum")
        whsum_ready = sem("whsum_ready")
        mean_psum = sem("mean_psum")
        d_x_in = sem("d_x_in")
        d_var = sem("d_var")
        d_ln = sem("d_ln")
        d_rstd = sem("d_rstd")
        d_hc = sem("d_hc")
        d_h = sem("d_h")
        d_hTp = sem("d_hTp")
        d_hT = sem("d_hT")
        d_whp = sem("d_whp")
        d_wh = sem("d_wh")
        d_dst_out = sem("d_dst_out")
        d_dst_in = sem("d_dst_in")
        d_adj_in = sem("d_adj_in")
        d_adj_free = sem("d_adj_free")
        d_z_ready = sem("d_z_ready")
        d_p_ready = sem("d_p_ready")
        d_zs = sem("d_zs")
        d_zTp = sem("d_zTp")
        d_zT = sem("d_zT")
        d_op = sem("d_op")
        d_acc = sem("d_acc")
        d_low = sem("d_low")
        d_ex = sem("d_ex")
        d_done = sem("d_done")
        d_out = sem("d_out")
        out_done = sem("out_done")

        gat_no = {0: 0, 1: 1, 3: 2}
        weights = {0: 1, 2: 2}

        def each_pair(eng, q, body):
            for u0, u1, slots, pre in RUNS[q]:
                def run(u):
                    body(u, slots, [BEFORE[q][i] + pre[i] + (u - u0 + 1) * slots[i] for i in range(2)])
                if u1 - u0 == 1:
                    run(u0)
                else:
                    with eng.Fori(u0, u1) as u:
                        run(u)

        def row(t3, k):
            return t3[:, bass.ds(k, 1), :].rearrange("p a f -> p (a f)")

        def col(t2, k):
            return t2[:, bass.ds(k, 1)]

        def first(n):
            return isinstance(n, int) and n == 0

        def from_first(eng, end, body):
            body(0)
            with eng.Fori(1, end) as n:
                body(n)

        block = ctx.enter_context(nc.Block())

        @block.sync
        def _(sp):
            def load_tile(t, i):
                sp.dma_start(adj_in[i][:, :], adj[bass.ds(t * P, P), :]).then_inc(adj_loaded[i], 16)

            sp.dma_start(x_nodes, x.rearrange("(t p) f -> p t f", p=P)).then_inc(x_loaded, 16)
            for i, (w, a) in enumerate(((w0, a0), (w1, a1), (w3, a3))):
                sp.dma_start(wcat[i][:, 0:F], w).then_inc(params, 16)
                sp.dma_start(acol[i][:, 0:1], a[F:2 * F, :]).then_inc(params, 16)
                sp.dma_start(acol[i][:, 1:2], a[0:F, :]).then_inc(params, 16)
            sp.dma_start(biasb[:, :], bias3.rearrange("(a f) -> a f", a=1).broadcast_to((P, F))).then_inc(params, 16)
            for t in range(3):
                load_tile(t, t)
            sp.wait_ge(wh4_taken, T // GROUP)
            table0 = tables[0].rearrange("(t p) c -> p t c", p=P)
            sp.dma_start(table0[:, :, 0:F], X[:, :, :]).then_inc(table0_out, 16)
            sp.dma_start(table0[:, :, F], dst[:, :], allow_slow_non_contiguous=True).then_inc(table0_out, 16)

            def three(v3):
                for j in range(3):
                    t = 3 * v3 + j
                    sp.wait_ge(narrowed, t + 1)
                    load_tile(t + 3, j)

            with sp.Fori(0, (T - 4) // 3) as v3:
                three(v3)
            sp.wait_ge(narrowed, T - 3)
            load_tile(T - 1, (T - 1) % 3)
            sp.wait_ge(table0_out, 32)
            for i in range(4):
                sp.wait_ge(scattered[i], 16 * T // 4)
            ordered = records_d.rearrange("(t p) c -> p t c", p=P)
            sp.dma_start(srec[:, 0:2, :], ordered[:, 0:2, 0:PART]).then_inc(first_in, 16)
            sp.dma_start(srec[:, 2:T, :], ordered[:, 2:T, 0:PART]).then_inc(sorted_in, 16)
            sp.dma_start(H[:, :, 0:F], ordered[:, :, PART:FEAT]).then_inc(sorted_in, 16)
            sp.dma_start(X[:, :, :], ordered[:, :, FEAT:REC]).then_inc(sorted_in, 16)
            sp.wait_ge(first_in, 16)
            sp.wait_ge(sorted_in, 48)

            sp.wait_ge(flag_ready, 1)
            dense = sp.value_load(flag[0:1, 0:1], min_val=0, max_val=1)
            with sp.If(dense > 0):
                sp.dma_start(X[:, :, :], x.rearrange("(t p) f -> p t f", p=P)).then_inc(d_x_in, 16)
                for n, (kind, _slope, _elu) in enumerate(LAYERS):
                    if kind == GAT:
                        g = gat_no[n]
                        sp.wait_ge(d_wh, (n + 1) * T)
                        sp.dma_start(dst_d[n].rearrange("a (t p) -> p (a t)", p=P), H[:, :, F:F + 1].rearrange("p t a -> p (t a)"),
                                     allow_slow_non_contiguous=True).then_inc(d_dst_out, 16)
                        sp.wait_ge(d_dst_out, 16 * (g + 1))
                        sp.dma_start(d_dst, dst_d[n].broadcast_to((P, N))).then_inc(d_dst_in, 16)
                    with sp.Fori(0, T) as t:
                        sp.wait_ge(d_adj_free, n * (T + 1) + t + 1)
                        sp.dma_start(d_adj[:, :], adj[bass.ds(t * P, P), :]).then_inc(d_adj_in, 16)
                sp.wait_ge(d_done, 4 * T)
                sp.dma_start(out.rearrange("(t p) f -> p t f", p=P), X[:, :, :]).then_inc(d_out, 16)
                sp.wait_ge(d_out, 16)
            with sp.Else():
                for q in (1, 2):
                    def store_pair(u, q=q):
                        for i in range(2):
                            k = 2 * u + i
                            sp.wait_ge(stage_ready, T * q + k + 1)
                            sp.dma_start(tables[q + 1][bass.ds(k * P, P), :], stage[i][:, 0:width[q + 1]]).then_inc(table_out[i], 16)

                    with sp.Fori(0, T // 2) as u:
                        store_pair(u)
                for i in range(2):
                    sp.wait_ge(table_out[i], 16 * 2 * (T // 2))

        @block.gpsimd
        def _(pool):
            steps = Steps(pool, pool_step)
            pool.memset(ident[:, :], 0.0).then_inc(pool_step, 1)
            pool.memset(ones[:, :], 1.0).then_inc(pool_step, 1)
            pool.memset(lower[:, :], 1.0).then_inc(pool_step, 1)
            pool.memset(epsc[:, :], EPS).then_inc(pool_step, 1)
            for c in range(NV):
                within = P * sum(b >= CAP - c for b in BOUNDS)
                pool.memset(limit[:, c:c + 1], float(within)).then_inc(pool_step, 1)
            pool.iota(colbase[:, :, :], pattern=[[N // 2, 2], [1, FC]], base=0, channel_multiplier=0,
                      allow_small_or_imprecise_dtypes=True).then_inc(pool_step, 1)
            pool.iota(bitcol[:, :], pattern=[[FC, FOLD]], base=N, channel_multiplier=0,
                      allow_small_or_imprecise_dtypes=True).then_inc(pool_step, 1)
            for q in range(FOLD):
                pool.memset(bitval[:, q:q + 1], 1 << q).then_inc(pool_step, 1)
            pool.iota(own, pattern=[[P, T]], base=0, channel_multiplier=1,
                      allow_small_or_imprecise_dtypes=True).then_inc(pool_step, 1)
            pool.iota(slot[:, :], pattern=[[1, CAP]], base=0, channel_multiplier=0,
                      allow_small_or_imprecise_dtypes=True).then_inc(pool_step, 1)
            pool.iota(degval[:, :], pattern=[[-1, NV]], base=CAP, channel_multiplier=0,
                      allow_small_or_imprecise_dtypes=True).then_inc(pool_step, 1)
            steps.at = 9 + NV + FOLD
            pool.wait_ge(pool_step, steps.at)
            steps.link(pool.affine_select(out=ident[:, :], in_=ident[:, :], compare_op=ALU.not_equal, fill=1.0,
                                          base=0, pattern=[[-1, P]], channel_multiplier=1))
            for q in range(FOLD):
                steps.link(pool.tensor_scalar(diag[:, q, :], ident[:, :], float(1 << q), None, ALU.mult))
            steps.link(pool.affine_select(out=lower[:, :], in_=lower[:, :], compare_op=ALU.is_gt, fill=0.0,
                                          base=0, pattern=[[1, P]], channel_multiplier=-1))
            pool.sem_inc(consts, 1)

            pool.wait_ge(table0_out, 32)
            def gather_early(w):
                for j in range(2):
                    u = 2 * w + j
                    pool.wait_ge(listed, u + 1)
                    if not first(w):
                        pool.wait_ge(early_free, u - 1)
                    pool.nop(nofuse=True)
                    for b in range(2 * EARLY):
                        pool.indirect_dma_start(
                            out=early[j][:, b, :], out_offset=None, in_=tables[0],
                            in_offset=bass.IndirectOffsetOnAxis(ap=early_ids[j][:, b // EARLY, b % EARLY:b % EARLY + 1], axis=0),
                        ).then_inc(early_in[j], 16)

            from_first(pool, T // 4, gather_early)

            with pool.Fori(0, T // 4) as t4:
                for i in range(4):
                    pool.wait_ge(rec_staged, 5 * (4 * t4 + i + 1))
                    pool.nop(nofuse=True)
                    pool.indirect_dma_start(out=records_d, out_offset=bass.IndirectOffsetOnAxis(ap=places[i][:, 0:1], axis=0),
                                            in_=recs[i][:, :], in_offset=None).then_inc(scattered[i], 16)

            pool.wait_ge(flag_ready, 1)
            dense = pool.value_load(flag[0:1, 0:1], min_val=0, max_val=1)
            with pool.If(dense > 0):
                pool.nop()
            with pool.Else():
                def wait_then_dma(s, value):
                    pool.wait_ge(s, value)
                    pool.nop(nofuse=True)

                def put(q, k, i):
                    pool.wait_ge(owns_ready, T * (q // 3) + k + 1)
                    wait_then_dma(stage_ready, T * q + k + 1)
                    to, cols = (tables[1], F + 2) if q == 0 else (out, F)
                    pool.indirect_dma_start(out=to, out_offset=bass.IndirectOffsetOnAxis(ap=owns[i][:, 0:1], axis=0),
                                            in_=stage[i][:, 0:cols], in_offset=None).then_inc(rows_out[i], 16)

                for q in range(4):
                    for i in range(2):
                        if q == 1:
                            pool.wait_ge(rows_out[i], 16 * (T // 2))
                        if q > 1:
                            pool.wait_ge(table_out[i], 16 * (q - 1) * (T // 2))

                    def pair(u, slots, _upto, q=q):
                        for i in range(2):
                            k = 2 * u + i
                            if slots[i]:
                                pool.wait_ge(ids_ready, T * q + k + 1)
                                if q or not isinstance(u, int) or u:
                                    pool.wait_ge(gather_free, T * q + k - 1)
                                pool.nop(nofuse=True)
                            skip, at = (EARLY, 1) if q == 0 else (0, 0)
                            for b in range(slots[i]):
                                pool.indirect_dma_start(
                                    out=gathered[i][:, at + b, 0:width[q]], out_offset=None, in_=tables[q],
                                    in_offset=bass.IndirectOffsetOnAxis(ap=ids[i][:, skip + b:skip + b + 1], axis=0),
                                ).then_inc(gather_in[i], 16)
                            if q in (0, 3) and not first(u):
                                put(q, k - 2, i)

                    each_pair(pool, q, pair)
                    if q in (0, 3):
                        for i in range(2):
                            put(q, T - 2 + i, i)
                for i in range(2):
                    pool.wait_ge(rows_out[i], 16 * 2 * (T // 2))

        @block.vector
        def _(dve):
            v = nc.vector
            steps = Steps(dve, dve_step)
            dve.wait_ge(consts, 1)
            link = steps.link
            dve.wait_ge(x_loaded, 16)

            def flat(t):
                return t.rearrange("p a b -> p (a b)")

            rows = (P, T, F)
            link(v.tensor_reduce(out=x_mean[:, :], in_=x_nodes, axis=AX.X, op=ALU.add))
            link(v.tensor_scalar(x_mean[:, :], x_mean[:, :], 1.0 / F, None, ALU.mult))
            v.tensor_tensor(X[:, :, :], x_nodes, x_mean[:, :].unsqueeze(2).broadcast_to(rows), ALU.subtract).then_inc(x_centred, 1)
            dve.wait_ge(x_squared, 1)
            v.tensor_reduce(out=x_var[:, :], in_=x_square, axis=AX.X, op=ALU.add).then_inc(x_summed, 1)
            dve.wait_ge(x_scaled, 1)

            def tiles(t3, g):
                return t3[:, bass.ds(GROUP * g, GROUP), :]

            def take_wh(g, i):
                dve.wait_ge(wh4_psum, g + 1)
                dve.nop(nofuse=True)
                wh4 = ps_fold[i][:, 0, :].rearrange("p (t c) -> p t c", c=P)
                v.tensor_copy(tiles(X, g), wh4[:, :, 0:F])
                v.tensor_copy(dst[:, bass.ds(GROUP * g, GROUP)], wh4[:, :, F])
                v.tensor_copy(node_src[:, bass.ds(GROUP * g, GROUP)], wh4[:, :, F + 1]).then_inc(wh4_taken, 1)

            def take_hT(g, i):
                dve.wait_ge(hT4_psum, g + 1)
                v.tensor_copy(hT4[i], ps_hT_b[i][:, :]).then_inc(hT4_ready, 1)

            def two_groups(g2):
                for i in range(2):
                    g = 2 * g2 + i
                    if not first(g2):
                        dve.wait_ge(hT4_psum, g - 1)
                    v.scalar_tensor_tensor(out=h4[i].rearrange("p (t f) -> p t f", f=F), in0=tiles(X, g), scalar=0.0,
                                           in1=x_rstd[:, bass.ds(GROUP * g, GROUP)].unsqueeze(2).broadcast_to((P, GROUP, F)),
                                           op0=ALU.max, op1=ALU.mult).then_inc(h4_ready, 1)
                    if not (first(g2) and i == 0):
                        take_hT(g - 1, 1 - i)
                    if not first(g2):
                        take_wh(g - 2, i)

            from_first(dve, T // GROUP // 2, two_groups)
            take_hT(T // GROUP - 1, 1)
            for i in range(2):
                take_wh(T // GROUP - 2 + i, i)
            dve.wait_ge(wh4_taken, T // GROUP)
            link(v.tensor_reduce(out=whsum[:, 0:F], in_=X[:, :, :].rearrange("p t f -> p f t"), axis=AX.X, op=ALU.add))
            dve.wait_ge(table0_out, 32)
            dve.sem_inc(whsum_ready, 1)
            dve.wait_ge(mean_psum, 1)
            steps.mark(v.tensor_scalar(meanb[:, :], ps_small[:, 0:F], 1.0 / N, None, ALU.mult))
            steps.mark(v.memset(zeros_s[:, :], 0.0))
            link(v.memset(whsum[:, :], 0.0))

            before = steps.total()
            EARLIES, SEARCH = 7, 2 + 2 * 5 + 6 + 2 * 5 + 6
            PAIR = EARLIES + SEARCH

            def largest(out, values, rest):
                for r in range(0, CAP, 8):
                    if r:
                        replaced = []
                        for i in range(2):
                            steps.after(found[i], alone=True)
                            replaced.append(steps.mark(v.match_replace(
                                out=rest[i], in_to_replace=out[i][:, r - 8:r], in_values=values[i], imm_value=0.0)))
                        values = rest
                    found = []
                    for i in range(2):
                        if r:
                            steps.after(replaced[i], alone=True)
                        found.append(steps.mark(v.max(out=out[i][:, r:r + 8], in_=values[i])))
                steps.after(found[1])

            merge = "p a k -> p (a k)"
            early_shape = (P, 2, EARLY)

            def early_scores(u, w, j):
                dve.wait_ge(early_in[j], 16 * 2 * EARLY * (w + 1))
                now = early_score[:, :, :]
                steps.link(v.scalar_tensor_tensor(
                    out=now, in0=early[j][:, :, F].rearrange("p (a k) -> p a k", a=2), scalar=-1.0,
                    in1=node_src[:, bass.ds(2 * u, 2)].unsqueeze(2).broadcast_to(early_shape), op0=ALU.mult, op1=ALU.subtract))
                steps.link(v.scalar_tensor_tensor(out=now, in0=now, scalar=LAYERS[0][1], in1=now, op0=ALU.mult, op1=ALU.min))
                steps.link(v.tensor_tensor(now, now, early_pad[j][:, :, :], ALU.add))
                steps.link(v.tensor_reduce(out=least[:, bass.ds(2 * u, 2)], in_=now, axis=AX.X, op=ALU.min))
                v.tensor_tensor(now, least[:, bass.ds(2 * u, 2)].unsqueeze(2).broadcast_to(early_shape), now,
                                ALU.subtract).then_inc(early_scored, 1)

            def early_rows(u, j):
                dve.wait_ge(early_weighted, u + 1)
                steps.mark(v.tensor_reduce(out=early_sum[:, :], in_=early_prob[:, :, :], axis=AX.X, op=ALU.add))
                v.tensor_tensor(early_prod, early[j][:, :, 0:F],
                                early_prob[:, :, :].rearrange(merge).unsqueeze(2).broadcast_to((P, 2 * EARLY, F)),
                                ALU.mult).then_inc(early_free, 1)
                dve.wait_ge(early_free, u + 1)
                steps.mark(v.tensor_reduce(out=X[:, bass.ds(2 * u, 2), :], in_=early_prod.rearrange("p (a k) f -> p a f k", a=2),
                                           axis=AX.X, op=ALU.add))
                steps.link(v.tensor_scalar(sum1[:, bass.ds(2 * u, 2)], early_sum[:, :], -1.0, None, ALU.add))

            def extract_pair(w, j):
                u = 2 * w + j
                steps.start(before + SEARCH * u if first(w) else before - 2 * EARLIES + PAIR * u)
                for i in range(2):
                    t = 2 * u + i
                    dve.wait_ge(folded, t + 1)
                    v.scalar_tensor_tensor(out=words[:, :], in0=flat(ps_fold[i][:, :, :]), scalar=float(N),
                                           in1=flat(colbase[:, :, :]), op0=ALU.mult, op1=ALU.add).then_inc(worded, 1)
                    dve.wait_ge(worded, t + 1)
                    dve.nop(nofuse=True)
                    for m in range(NSEG):
                        found = v.max(out=cand[:, i, m * 8:(m + 1) * 8], in_=words[:, m * SEG:(m + 1) * SEG])
                    steps.link(found, alone=True)
                largest([most[:, i, :] for i in range(2)], [cand[:, i, :] for i in range(2)],
                        [left[:, i, :] for i in range(2)])
                if not first(w):
                    early_scores(u - 2, w - 1, j)
                steps.link(v.tensor_copy(mosti[:, :, :], most[:, :, :]))
                word = steps.mark(v.tensor_scalar(wordi[:, :, :], mosti[:, :, :], N.bit_length() - 1, None, ALU.logical_shift_right))
                base = steps.mark(v.tensor_scalar(basei[:, :, :], mosti[:, :, :], N - 1, None, ALU.bitwise_and))
                pairs = (P, 2 * CAP, FOLD)
                merged = "p a c q -> p (a c) q"
                steps.after(word)
                steps.mark(v.tensor_tensor(bits[:, :, :, :].rearrange(merged), flat(wordi[:, :, :]).unsqueeze(2).broadcast_to(pairs),
                                           bitval[:, :].unsqueeze(1).broadcast_to(pairs), ALU.bitwise_and))
                steps.after(base)
                steps.link(v.tensor_tensor(edge[:, :, :, :].rearrange(merged), flat(basei[:, :, :]).unsqueeze(2).broadcast_to(pairs),
                                           bitcol[:, :].unsqueeze(1).broadcast_to(pairs), ALU.add))
                whole = "p a c q -> p (a c q)"
                steps.link(v.scalar_tensor_tensor(out=edge[:, :, :, :].rearrange(whole), in0=bits[:, :, :, :].rearrange(whole),
                                                  scalar=0.0, in1=edge[:, :, :, :].rearrange(whole),
                                                  op0=ALU.is_gt, op1=ALU.mult), alone=True)
                largest([best[:, i, :] for i in range(2)], [flat(edge[:, i, :, :]) for i in range(2)],
                        [flat(rest[:, i, :, :]) for i in range(2)])
                ownb = own[:, bass.ds(2 * u, 2)].unsqueeze(2).broadcast_to((P, 2, CAP))
                steps.mark(v.tensor_scalar(valid[:, :, :], best[:, :, :], float(N), None, ALU.is_ge))
                steps.link(v.scalar_tensor_tensor(out=nbr[:, :, :], in0=best[:, :, :], scalar=-float(N), in1=ownb,
                                                  op0=ALU.add, op1=ALU.subtract))
                steps.link(v.tensor_tensor(nbr[:, :, :], nbr[:, :, :], valid[:, :, :], ALU.mult))
                steps.mark(v.tensor_tensor(top[:, bass.ds(2 * u, 2), :], nbr[:, :, :], ownb, ALU.add))
                steps.mark(v.tensor_scalar(early_pad[j][:, :, :], valid[:, :, 0:EARLY], -PAD, PAD, ALU.mult, ALU.add))
                steps.mark(v.tensor_reduce(out=deg[:, bass.ds(2 * u, 2)], in_=valid[:, :, :], axis=AX.X, op=ALU.add))
                v.tensor_tensor(early_ids[j][:, :, :], nbr[:, :, 0:EARLY],
                                own[:, bass.ds(2 * u, 2)].unsqueeze(2).broadcast_to(early_shape), ALU.add).then_inc(listed, 1)
                if not first(w):
                    early_rows(u - 2, j)
                dve.wait_ge(listed, u + 1)
                dve.nop(nofuse=True)
                assert steps.at == (SEARCH if first(w) else PAIR), steps.at

            def extract_two(w):
                for j in range(2):
                    extract_pair(w, j)

            from_first(dve, T // 4, extract_two)
            steps.start(before - 2 * EARLIES + PAIR * (T // 2))

            link(v.tensor_tensor(is_v, deg.unsqueeze(1).broadcast_to((P, NV, T)),
                                 degval[:, :].unsqueeze(2).broadcast_to((P, NV, T)), ALU.is_equal))
            v.tensor_reduce(out=cnt[:, :], in_=is_v, axis=AX.X, op=ALU.add).then_inc(cnt_ready, 1)
            dve.wait_ge(cnt_ready, 1)
            steps.mark(v.tensor_tensor_scan(cpre[:, :], cnt[:, :], zeros_s[:, :], 0.0, ALU.add, ALU.add))
            link(v.tensor_tensor_scan(flat(run_v), flat(is_v), zeros_s[:, 0:1].broadcast_to((P, NV * T)), 0.0, ALU.add, ALU.add))
            dve.wait_ge(cnt_summed, 1)
            steps.mark(v.tensor_tensor(cpre[:, :], cpre[:, :], cnt[:, :], ALU.subtract))
            link(v.tensor_tensor_scan(tpre[:, :], ps_small[:, W:W + NV], zeros_s[:, :], 0.0, ALU.add, ALU.add))
            link(v.tensor_tensor(base_v[:, :], tpre[:, :], ps_small[:, W:W + NV], ALU.subtract))
            link(v.tensor_tensor(base_v[:, :], base_v[:, :], ps_small[:, 0:NV], ALU.add))
            link(v.tensor_tensor(base_v[:, :], base_v[:, :], cpre[:, :], ALU.subtract))
            link(v.tensor_tensor(run_v, run_v, base_v[:, :].unsqueeze(2).broadcast_to((P, NV, T)), ALU.add))
            link(v.tensor_tensor(run_v, run_v, is_v, ALU.mult))
            link(v.tensor_reduce(out=rankv[:, :], in_=run_v.rearrange("p v t -> p t v"), axis=AX.X, op=ALU.add))
            v.tensor_scalar(rank[:, :], rankv[:, :], -1.0, None, ALU.add).then_inc(ranked, 1)
            for j in range(2):
                early_scores(T // 2 - 2 + j, T // 4 - 1, j)
                early_rows(T // 2 - 2 + j, j)
            dve.sem_inc(early_done, 1)

            steps.mark(v.tensor_tensor(over[:, :], total[:, :], deg, ALU.not_equal))
            link(v.tensor_tensor(over_v[:, :], tpre[:, :], limit[:, :], ALU.is_gt))
            steps.mark(v.tensor_reduce(out=over1[:, 0:1], in_=over[:, :], axis=AX.X, op=ALU.max))
            link(v.tensor_reduce(out=over1[:, 1:2], in_=over_v[:, :], axis=AX.X, op=ALU.max))
            v.tensor_tensor(over1[:, 0:1], over1[:, 0:1], over1[:, 1:2], ALU.max).then_inc(over_ready, 1)
            dve.wait_ge(over_summed, 1)
            v.tensor_scalar(flag[:, :], ps_small[0:1, 0:1], 0.0, None, ALU.is_gt).then_inc(flag_ready, 1)

            dve.wait_ge(flag_ready, 1)
            after_rank = steps.total()
            dense = dve.value_load(flag[0:1, 0:1], min_val=0, max_val=1)
            with dve.If(dense > 0):
                done = after_rank
                dve.wait_ge(d_x_in, 16)
                for n, (kind, slope, elu) in enumerate(LAYERS):
                    g = gat_no.get(n)
                    PREP = 1
                    with dve.Fori(0, T) as t:
                        steps.start(done + PREP * t)
                        steps.link(v.bn_stats(out=bn[:, :], in_=row(X, t)), alone=True)
                        v.bn_aggr(out=mv[0][:, :], in_=bn[:, :]).then_inc(d_var, 1)
                        dve.wait_ge(d_rstd, n * T + t + 1)
                        v.tensor_scalar(hc[0][:, :], row(X, t), mv[0][:, 0:1], 0.0, ALU.subtract, ALU.max).then_inc(d_hc, 1)
                        if kind == GAT:
                            dve.wait_ge(d_whp, g * T + t + 1)
                            v.tensor_copy(row(H, t), ps_wh[0]).then_inc(d_wh, 1)
                        else:
                            dve.wait_ge(d_h, n * T + t + 1)
                            v.tensor_copy(row(H, t)[:, 0:F], h[0][:, :]).then_inc(d_wh, 1)
                        dve.wait_ge(d_wh, n * T + t + 1)
                        dve.nop(nofuse=True)
                        assert steps.at == PREP
                    done = done + PREP * T
                    if kind == GAT:
                        dve.wait_ge(d_dst_in, 16 * (g + 1))
                    dve.sem_inc(d_adj_free, 1)

                    ROWS = {0: 9, 1: 9, 2: 2, 3: 9}[n]
                    with dve.Fori(0, T) as t:
                        steps.start(done + ROWS * t)
                        dve.wait_ge(d_adj_in, 16 * (n * T + t + 1))
                        if kind == GAT:
                            link = steps.link
                            link(v.tensor_scalar(d_z, d_dst, row(H, t)[:, F + 1:F + 2], None, ALU.add))
                            link(v.scalar_tensor_tensor(out=d_z, in0=d_z, scalar=slope, in1=d_z, op0=ALU.mult, op1=ALU.max))
                            link(v.scalar_tensor_tensor(out=d_t, in0=d_adj[:, :], scalar=0.0, in1=d_z,
                                                        op0=ALU.is_gt, op1=ALU.mult))
                            v.tensor_scalar(d_z, d_adj[:, :], 0.0, NEG_INF[n], ALU.is_le, ALU.mult).then_inc(d_adj_free, 1)
                            dve.wait_ge(d_adj_free, n * (T + 1) + t + 2)
                            link(v.tensor_tensor(d_z, d_z, d_t, ALU.add))
                            link(v.tensor_reduce(out=nmax[1][:, :], in_=d_z, axis=AX.X, op=ALU.max))
                            v.tensor_scalar(nmax[0][:, :], nmax[1][:, :], -1.0, None, ALU.mult).then_inc(d_z_ready, 1)
                            dve.wait_ge(d_p_ready, g * T + t + 1)
                        else:
                            v.tensor_scalar(d_z, d_adj[:, :], 1.0, None, ALU.is_equal).then_inc(d_adj_free, 1)
                            dve.wait_ge(d_adj_free, n * (T + 1) + t + 2)
                            dve.sem_inc(d_z_ready, 1)
                        steps.link(v.memset(acc[0][:, :], 0.0), alone=True)
                        with dve.Fori(0, T // 4) as gr:
                            dve.wait_ge(d_op, (n * T + t) * (T // 4) + gr + 1)
                            v.tensor_tensor(acc[0][:, :], acc[0][:, :], ps_o, ALU.add).then_inc(d_acc, 1)
                            dve.wait_ge(d_acc, (n * T + t) * (T // 4) + gr + 1)
                            dve.nop(nofuse=True)
                        if kind == SUM:
                            steps.link(v.tensor_tensor(acc[0][:, :], acc[0][:, :], row(H, t)[:, 0:F], ALU.add))
                            v.tensor_tensor(row(X, t), row(X, t), acc[0][:, :], ALU.add).then_inc(d_done, 1)
                        else:
                            steps.link(v.reciprocal(rinv[:, :], rsum[0][:, :]))
                            steps.link(v.tensor_scalar(hp[0][:, :], acc[0][:, :], rinv[:, 0:1], None, ALU.mult))
                            if elu:
                                v.tensor_scalar(low[0][:, :], hp[0][:, :], 0.0, None, ALU.min).then_inc(d_low, 1)
                                dve.wait_ge(d_ex, g * T + t + 1)
                                steps.link(v.scalar_tensor_tensor(out=tmp[:, :], in0=hp[0][:, :], scalar=0.0, in1=ex[0][:, :],
                                                                  op0=ALU.max, op1=ALU.add))
                                v.scalar_tensor_tensor(out=row(X, t), in0=tmp[:, :], scalar=-1.0, in1=row(X, t),
                                                       op0=ALU.add, op1=ALU.add).then_inc(d_done, 1)
                            else:
                                steps.link(v.tensor_tensor(tmp[:, :], hp[0][:, :], biasb[:, :], ALU.add))
                                v.tensor_tensor(row(X, t), row(X, t), tmp[:, :], ALU.add).then_inc(d_done, 1)
                        dve.wait_ge(d_done, n * T + t + 1)
                        dve.nop(nofuse=True)
                        assert steps.at == ROWS, (n, steps.at)
                    done = done + ROWS * T
            with dve.Else():
                steps.start(after_rank)
                link = steps.link
                dve.wait_ge(first_in, 16)
                dve.wait_ge(sorted_in, 48)
                for i in range(2):
                    steps.mark(v.memset(pads[i][:, 0:1], 0.0))
                steps.mark(v.tensor_copy(src[:, :], srec[:, :, SRC]))
                link(v.tensor_copy(sdeg, srec[:, :, DEG]))
                slotb = slot[:, :].unsqueeze(1).broadcast_to((P, T, CAP))
                sdegb = sdeg.unsqueeze(2).broadcast_to((P, T, CAP))
                link(v.tensor_tensor(pad, slotb, sdegb, ALU.is_ge))
                v.tensor_scalar(pad, pad, PAD, None, ALU.mult).then_inc(masks_ready, 1)
                steps.mark(v.tensor_tensor(once, slotb, sdegb, ALU.is_lt))
                steps.mark(v.tensor_scalar(nonempty[:, :], sdeg, 0.0, None, ALU.is_gt))
                link(v.tensor_scalar(empty[:, :], sdeg, 0.0, None, ALU.is_equal))

                done = steps.total()
                for q, (kind, slope, elu) in enumerate(LAYERS):
                    last = q == 3
                    SCORES = {0: 2, 1: 3, 2: 0, 3: 2}[q]
                    ROWSUM = {0: 6, 1: 5, 2: 1, 3: 5}[q]
                    UPDATE = 1 if last else 3
                    STORE = 0 if last else (1 if q == 1 else 2)
                    PER = SCORES + ROWSUM + UPDATE + STORE

                    def scores(q, k, i, slots):
                        g = gathered[i]
                        dve.wait_ge(pads_ready, T * q + k + 1)
                        if q == 1:
                            steps.mark(v.tensor_copy(row(srec, k)[:, 0:slots], g[:, 0:slots, RANK]))
                        new = slice(1 if q == 0 else 0, slots)
                        if q == 0 and slots == 1:
                            dve.sem_inc(dve_step, SCORES)
                            steps.at += SCORES
                            dve.nop(nofuse=True)
                        else:
                            steps.link(v.tensor_scalar(score[i][:, new], g[:, new, F], -1.0,
                                                       col(src, k), ALU.mult, ALU.subtract))
                            steps.link(v.scalar_tensor_tensor(out=score[i][:, new], in0=score[i][:, new], scalar=slope,
                                                              in1=score[i][:, new], op0=ALU.mult, op1=ALU.min), alone=True)
                        v.tensor_tensor_reduce(out=score[i][:, 0:slots], in0=score[i][:, 0:slots],
                                               in1=pads[i][:, 0:slots], scale=1.0, scalar=BIG, op0=ALU.add,
                                               op1=ALU.min, accum_out=nmax[i][:, :]).then_inc(score_ready, 1)

                    def rowsum(q, k, i, slots):
                        g = gathered[i]
                        if kind == GAT:
                            dve.wait_ge(prob_ready, T * gat_no[q] + k + 1)
                            weight = prob[i][:, 0:slots]
                        else:
                            weight = row(once, k)[:, 0:slots]
                        v.tensor_tensor(prod[:, 0:slots, :], g[:, 0:slots, 0:F],
                                        weight.unsqueeze(2).broadcast_to((P, slots, F)), ALU.mult).then_inc(gather_free, 1)
                        if kind == GAT:
                            total_w = rsum[i]
                            if q == 0:
                                total_w = rtot
                                steps.link(v.scalar_tensor_tensor(out=rtot[:, :], in0=row(srec, k)[:, SUM1:SUM1 + 1],
                                                                  scalar=prob[i][:, 0:1], in1=rsum[i][:, :],
                                                                  op0=ALU.mult, op1=ALU.add))
                            inverse = steps.mark(v.reciprocal(rinv[:, :], total_w[:, :]))
                            steps.mark(v.tensor_scalar(fill[:, :], meanb[:, :], col(empty, k), None, ALU.mult))
                            steps.after(inverse)
                            steps.mark(v.tensor_tensor(rinv[:, :], rinv[:, :], col(nonempty, k), ALU.mult))
                        dve.wait_ge(gather_free, T * q + k + 1)
                        steps.link(v.tensor_reduce(out=acc[i][:, :], in_=prod[:, 0:slots, :].rearrange("p b f -> p f b"),
                                                   axis=AX.X, op=ALU.add))
                        if kind == GAT:
                            steps.link(v.scalar_tensor_tensor(out=hp[i][:, :], in0=acc[i][:, :], scalar=rinv[:, 0:1],
                                                              in1=fill[:, :], op0=ALU.mult, op1=ALU.add))
                            if elu:
                                v.tensor_scalar(low[i][:, :], hp[i][:, :], 0.0, None, ALU.min).then_inc(low_ready, 1)

                    def update(q, k, i):
                        if kind == SUM:
                            steps.link(v.tensor_tensor(tmp[:, :], acc[i][:, :], row(H, k)[:, 0:F], ALU.add))
                            steps.link(v.tensor_tensor(row(X, k), row(X, k), tmp[:, :], ALU.add))
                        elif elu:
                            dve.wait_ge(ex_ready, T * gat_no[q] + k + 1)
                            steps.link(v.scalar_tensor_tensor(out=tmp[:, :], in0=hp[i][:, :], scalar=0.0, in1=ex[i][:, :],
                                                              op0=ALU.max, op1=ALU.add))
                            steps.link(v.scalar_tensor_tensor(out=row(X, k), in0=tmp[:, :], scalar=-1.0, in1=row(X, k),
                                                              op0=ALU.add, op1=ALU.add))
                        else:
                            steps.link(v.tensor_tensor(tmp[:, :], hp[i][:, :], biasb[:, :], ALU.add))
                            if isinstance(k, int) and k < 2:
                                dve.wait_ge(table_out[i], 16 * (T // 2 * 2))
                            else:
                                dve.wait_ge(rows_out[i], 16 * (T // 2) + 8 * (k - i))
                            v.tensor_tensor(stage[i][:, 0:F], row(X, k), tmp[:, :], ALU.add).then_inc(stage_ready, 1)
                        if not last:
                            dve.nop(nofuse=True)
                            steps.link(v.bn_stats(out=bn[:, :], in_=row(X, k)), alone=True)
                            v.bn_aggr(out=mv[i][:, :], in_=bn[:, :]).then_inc(var_ready, 1)
                            dve.wait_ge(var_ready, T * q + k + 1)
                            v.tensor_scalar(hc[i][:, :], row(X, k), mv[i][:, 0:1], 0.0, ALU.subtract, ALU.max).then_inc(hc_ready, 1)

                    def store(q, k, i):
                        start = isinstance(k, int) and k < 2
                        if q == 0 and not start:
                            dve.wait_ge(rows_out[i], 8 * (k - i))
                        elif q == 1 and start:
                            dve.wait_ge(rows_out[i], 16 * (T // 2))
                        elif q:
                            dve.wait_ge(table_out[i], 16 * (T // 2 * (q - 1)) + 8 * (k - i))
                        if q == 1:
                            dve.wait_ge(h_ready, T * q + k + 1)
                            v.tensor_copy(stage[i][:, 0:F], h[i][:, :]).then_inc(stage_ready, 1)
                            steps.mark(v.tensor_copy(row(H, k)[:, 0:F], h[i][:, :]))
                        else:
                            dve.wait_ge(wh_psum, T * (q // 2) + k + 1)
                            if q == 0:
                                v.tensor_copy(stage[i][:, 0:F + 1], ps_wh[i][:, 0:F + 1])
                                v.tensor_copy(stage[i][:, RANK:RANK + 1], col(own, k)).then_inc(stage_ready, 1)
                            else:
                                v.tensor_copy(stage[i][:, :], ps_wh[i]).then_inc(stage_ready, 1)
                            steps.mark(v.tensor_copy(col(src, k), ps_wh[i][:, F + 1:F + 2]))
                            steps.mark(v.tensor_tensor(whsum[:, :], whsum[:, :], ps_wh[i], ALU.add))

                    def tile(k, i, slots, upto):
                        if q == 0:
                            slots = slots + 1
                        dve.wait_ge(gather_in[i], 16 * upto)
                        if kind == GAT:
                            scores(q, k, i, slots)
                        if not (isinstance(k, int) and k < 2) and not last:
                            store(q, k - 2, i)
                        if not (isinstance(k, int) and k == 0):
                            update(q, k - 1, 1 - i)
                        rowsum(q, k, i, slots)

                    def pair(u, slots, upto):
                        for i in range(2):
                            k = 2 * u + i
                            if isinstance(k, int) and k < 2:
                                steps.start(done + (PER - UPDATE - STORE if k else 0))
                                tile(k, i, slots[i], upto[i])
                                assert steps.at == PER - STORE - (0 if k else UPDATE), (q, steps.at)
                            else:
                                steps.start(done - UPDATE - 2 * STORE + PER * k)
                                tile(k, i, slots[i], upto[i])
                                assert steps.at == PER, (q, steps.at)

                    each_pair(dve, q, pair)
                    steps.start(done - UPDATE - 2 * STORE + PER * T)
                    update(q, T - 1, 1)
                    if not last:
                        store(q, T - 2, 0)
                        steps.after(steps.at)
                        store(q, T - 1, 1)
                    assert steps.at == UPDATE + 2 * STORE
                    done = done + PER * T
                    if q in weights:
                        dve.wait_ge(dve_step, done)
                        dve.sem_inc(whsum_ready, 1)
                        dve.wait_ge(mean_psum, weights[q] + 1)
                        steps.start(done)
                        steps.link(v.tensor_scalar(meanb[:, :], ps_small[:, 0:F], 1.0 / N, None, ALU.mult))
                        steps.link(v.memset(whsum[:, :], 0.0))
                        done = done + 2

        @block.scalar
        def _(act):
            s = nc.scalar
            act.preload_act_table_set("natural_log_exp_and_others")
            for i in range(3):
                act.wait_ge(w_t, i + 1)
                s.copy(wT[i][:, :], ps_hT[0][:, 0:F]).then_inc(w_tc, 1)
            for i in range(3):
                act.wait_ge(w_a, i + 1)
                s.copy(wcat[i][:, F:W], ps_hT[1][:, 0:2]).then_inc(w_ready, 1)

            def normalise(n, k, i, p=None):
                act.wait_ge(var_ready, n + k + 1)
                s.activation(lnv[i][:, :], mv[i][:, 1:2], ACT.Ln, bias=epsc[:, 0:1]).then_inc(ln_ready, 1)
                act.wait_ge(ln_ready, n + k + 1)
                s.activation(rstd[i][:, :], lnv[i][:, :], ACT.Exp, scale=-0.5).then_inc(rstd_ready, 1)
                act.wait_ge(rstd_ready, n + k + 1)
                act.wait_ge(hc_ready, n + k + 1)
                s.activation(h[i][:, :], hc[i][:, :], ACT.Copy, scale=rstd[i][:, 0:1]).then_inc(h_ready, 1)
                if p is not None:
                    act.wait_ge(hT_psum, p + k + 1)
                    s.copy(hT[i][:, :], ps_hT[i]).then_inc(hT_ready, 1)

            act.wait_ge(x_centred, 1)
            s.activation(x_square, X[:, :, :], ACT.Square).then_inc(x_squared, 1)
            act.wait_ge(x_summed, 1)
            s.activation(x_mean[:, :], x_var[:, :], ACT.Ln, scale=1.0 / F, bias=epsc[:, 0:1]).then_inc(x_squared, 1)
            act.wait_ge(x_squared, 2)
            s.activation(x_rstd[:, :], x_mean[:, :], ACT.Exp, scale=-0.5).then_inc(x_scaled, 1)

            def weigh_early(u):
                act.wait_ge(early_scored, u + 1)
                s.activation(early_prob[:, :, :], early_score[:, :, :], ACT.Exp).then_inc(early_weighted, 1)

            def six(v6):
                for j in range(0, 6, 2):
                    t = 6 * v6 + j
                    for i in range(2):
                        act.wait_ge(adj_loaded[(j + i) % 3], 16 * (2 * v6 + (j + i) // 3 + 1))
                        if not (first(v6) and j == 0):
                            act.wait_ge(folded, t + i - 1)
                        s.activation(adj_bf[:, i, :], adj_in[(j + i) % 3][:, :], ACT.Relu,
                                     accum_out=col(total, t + i)).then_inc(narrowed, 1)
                        if i == 0 and not first(v6):
                            weigh_early(3 * v6 + j // 2 - 3)

            from_first(act, (T - 4) // 6, six)
            for t in range(T - 4, T):
                act.wait_ge(adj_loaded[t % 3], 16 * (t // 3 + 1))
                act.wait_ge(folded, t - 1)
                s.activation(adj_bf[:, t % 2, :], adj_in[t % 3][:, :], ACT.Relu, accum_out=col(total, t)).then_inc(narrowed, 1)
                if t % 2 == 0:
                    weigh_early(t // 2 - 3)
            for u in range(T // 2 - 3, T // 2):
                weigh_early(u)

            act.wait_ge(ranked, 1)
            def stage_records(t4):
                for i in range(4):
                    t = 4 * t4 + i
                    if not first(t4):
                        act.wait_ge(scattered[i], 16 * t4)
                    s.copy(recs[i][:, 0:CAP], row(top, t)).then_inc(rec_staged, 1)
                    s.copy(recs[i][:, PART:FEAT], row(X, t)).then_inc(rec_staged, 1)
                    s.copy(recs[i][:, CAP:PART], nodes[:, :, bass.ds(t, 1)].rearrange("p c t -> p (c t)")).then_inc(rec_staged, 1)
                    s.copy(recs[i][:, FEAT:REC], row(x_nodes, t)).then_inc(rec_staged, 1)
                    s.copy(places[i][:, :], col(rank, t)).then_inc(rec_staged, 1)

            act.wait_ge(early_done, 1)
            from_first(act, T // 4, stage_records)

            act.wait_ge(flag_ready, 1)
            dense = act.value_load(flag[0:1, 0:1], min_val=0, max_val=1)

            with act.If(dense > 0):
                for n, (kind, _slope, elu) in enumerate(LAYERS):
                    g = gat_no.get(n)
                    with act.Fori(0, T) as t:
                        act.wait_ge(d_var, n * T + t + 1)
                        s.activation(lnv[0][:, :], mv[0][:, 1:2], ACT.Ln, bias=epsc[:, 0:1]).then_inc(d_ln, 1)
                        act.wait_ge(d_ln, n * T + t + 1)
                        s.activation(rstd[0][:, :], lnv[0][:, :], ACT.Exp, scale=-0.5).then_inc(d_rstd, 1)
                        act.wait_ge(d_rstd, n * T + t + 1)
                        act.wait_ge(d_hc, n * T + t + 1)
                        s.activation(h[0][:, :], hc[0][:, :], ACT.Copy, scale=rstd[0][:, 0:1]).then_inc(d_h, 1)
                        if kind == GAT:
                            act.wait_ge(d_hTp, g * T + t + 1)
                            s.copy(hT[0][:, :], ps_hT[0]).then_inc(d_hT, 1)
                    with act.Fori(0, T) as t:
                        if kind == GAT:
                            act.wait_ge(d_z_ready, n * T + t + 1)
                            s.activation(d_z, d_z, ACT.Exp, bias=nmax[0][:, 0:1], accum_out=rsum[0][:, 0:1]).then_inc(d_p_ready, 1)
                            act.wait_ge(d_p_ready, g * T + t + 1)
                        else:
                            act.wait_ge(d_z_ready, n * T + t + 1)
                        with act.Fori(0, T // 4) as gr:
                            s.copy(zs, d_z[:, bass.ds(gr * (4 * P), 4 * P)]).then_inc(d_zs, 1)
                            act.wait_ge(d_zTp, (n * T + t) * (T // 4) + gr + 1)
                            s.copy(zT, ps_z).then_inc(d_zT, 1)
                            act.wait_ge(d_acc, (n * T + t) * (T // 4) + gr + 1)
                        if elu:
                            act.wait_ge(d_low, g * T + t + 1)
                            s.activation(ex[0][:, :], low[0][:, :], ACT.Exp).then_inc(d_ex, 1)
            with act.Else():
                def stage_ids(k, i):
                    s.copy(ids[i][:, :], row(srec, k)[:, 0:CAP]).then_inc(ids_ready, 1)

                def stage_pads(q, k, i):
                    if q == 0:
                        if not (isinstance(k, int) and k < 2):
                            act.wait_ge(gather_free, k - 1)
                        s.copy(gathered[i][:, 0, 0:F], row(H, k)[:, 0:F])
                        s.copy(score[i][:, 0:1], row(srec, k)[:, LEAST:LEAST + 1])
                        s.copy(pads[i][:, 1:CAP - EARLY + 1], row(pad, k)[:, EARLY:CAP]).then_inc(pads_ready, 1)
                    else:
                        s.copy(pads[i][:, :], row(pad, k)).then_inc(pads_ready, 1)

                act.wait_ge(first_in, 16)
                stage_ids(0, 0)
                stage_ids(1, 1)
                act.wait_ge(masks_ready, 1)
                act.wait_ge(sorted_in, 48)
                stage_pads(0, 0, 0)
                stage_pads(0, 1, 1)
                for q, (kind, _slope, elu) in enumerate(LAYERS):
                    last = q == 3
                    proj = None if q == 1 else T * (q // 2)

                    def pair(u, slots, upto, q=q, kind=kind, elu=elu, last=last, proj=proj):
                        for i in range(2):
                            k = 2 * u + i
                            start = isinstance(u, int) and u == 0
                            if kind == GAT:
                                act.wait_ge(score_ready, T * gat_no[q] + k + 1)
                                n = slots[i] + (1 if q == 0 else 0)
                                s.activation(prob[i][:, 0:n], score[i][:, 0:n], ACT.Exp, bias=nmax[i][:, 0:1],
                                             scale=-1.0, accum_out=rsum[i][:, 0:1]).then_inc(prob_ready, 1)
                            if not last and not (start and i == 0):
                                normalise(T * q, k - 1, 1 - i, proj)
                            if elu:
                                act.wait_ge(low_ready, T * gat_no[q] + k + 1)
                                s.activation(ex[i][:, :], low[i][:, :], ACT.Exp).then_inc(ex_ready, 1)
                            if not (last and isinstance(u, int) and u == T // 2 - 1):
                                act.wait_ge(gather_in[i], 16 * upto[i])
                                end = isinstance(u, int) and u == T // 2 - 1
                                nxt = i if end else k + 2
                                stage_ids(nxt, i)
                                stage_pads(q + end, nxt, i)
                            if q in (0, 3):
                                if last or not start:
                                    act.wait_ge(rows_out[i], 16 * (T // 2 * (q // 3) + u))
                                s.copy(owns[i][:, :], row(srec, k)[:, OWN:OWN + 1]).then_inc(owns_ready, 1)

                    each_pair(act, q, pair)
                    if not last:
                        normalise(T * q, T - 1, 1, proj)

        @block.tensor
        def _(pe):
            mm = nc.tensor.matmul
            pe.wait_ge(consts, 1)
            pe.wait_ge(params, 16 * 10)
            for i in range(3):
                if i:
                    pe.wait_ge(w_tc, i)
                nc.tensor.transpose(ps_hT[0][:, 0:F], wcat[i][:, 0:F], ident[0:F, 0:F]).then_inc(w_t, 1)
            for i in range(3):
                pe.wait_ge(w_tc, i + 1)
                if i:
                    pe.wait_ge(w_ready, i)
                mm(ps_hT[1][:, 0:2], wT[i][:, :], acol[i][:, :], start=True, stop=True).then_inc(w_a, 1)
            pe.wait_ge(w_ready, 3)

            def project(n, p, w, k, i):
                pe.wait_ge(h_ready, n + k + 1)
                pe.nop(nofuse=True)
                nc.tensor.transpose(ps_hT[i], h[i][:, :], ident[:, :]).then_inc(hT_psum, 1)
                pe.wait_ge(hT_ready, p + k + 1)
                mm(ps_wh[i], hT[i][:, :], wcat[w][:, :], start=True, stop=True).then_inc(wh_psum, 1)

            def project_group(g, i):
                pe.wait_ge(hT4_ready, g + 1)
                if not (isinstance(g, int) and g < 2):
                    pe.wait_ge(wh4_taken, g - 1)
                for c in range(GROUP):
                    done = mm(ps_fold[i][:, 0, c * P:c * P + W], hT4[i][:, c * P:(c + 1) * P], wcat[0][:, :], start=True, stop=True)
                done.then_inc(wh4_psum, 1)

            def two_groups(g2):
                for i in range(2):
                    g = 2 * g2 + i
                    pe.wait_ge(h4_ready, g + 1)
                    if not first(g2):
                        pe.wait_ge(hT4_ready, g - 1)
                    pe.nop(nofuse=True)
                    for c in range(GROUP):
                        done = nc.tensor.transpose(ps_hT_b[i][:, c * P:(c + 1) * P], h4[i][:, c * F:(c + 1) * F], ident[:, :])
                    done.then_inc(hT4_psum, 1)
                    if not (first(g2) and i == 0):
                        project_group(g - 1, 1 - i)

            from_first(pe, T // GROUP // 2, two_groups)
            project_group(T // GROUP - 1, 1)
            pe.wait_ge(whsum_ready, 1)
            mm(ps_small[:, 0:F], ones[:, :], whsum[:, 0:F], start=True, stop=True).then_inc(mean_psum, 1)

            def fold_pair(u):
                for i in range(2):
                    t = 2 * u + i
                    pe.wait_ge(narrowed, t + 1)
                    if not first(u):
                        pe.wait_ge(worded, t - 1)
                    for half in range(2):
                        for q in range(FOLD):
                            c = half * (N // 2) + q * FC
                            done = mm(ps_fold[i][:, half, :], diag[:, q, :], adj_bf[:, i, c:c + FC],
                                      start=q == 0, stop=q == FOLD - 1)
                    done.then_inc(folded, 1)

            from_first(pe, T // 2, fold_pair)
            pe.wait_ge(cnt_ready, 1)
            mm(ps_small[:, 0:NV], lower[:, :], cnt[:, :], start=True, stop=True)
            mm(ps_small[:, W:W + NV], ones[:, :], cnt[:, :], start=True, stop=True).then_inc(cnt_summed, 1)
            pe.wait_ge(over_ready, 1)
            mm(ps_small[:, 0:1], ones[:, :], over1[:, 0:1], start=True, stop=True).then_inc(over_summed, 1)

            pe.wait_ge(flag_ready, 1)
            dense = pe.value_load(flag[0:1, 0:1], min_val=0, max_val=1)
            with pe.If(dense > 0):
                for n, (kind, _slope, _elu) in enumerate(LAYERS):
                    g = gat_no.get(n)
                    if kind == GAT:
                        with pe.Fori(0, T) as t:
                            pe.wait_ge(d_h, n * T + t + 1)
                            pe.nop(nofuse=True)
                            nc.tensor.transpose(ps_hT[0], h[0][:, :], ident[:, :]).then_inc(d_hTp, 1)
                            pe.wait_ge(d_hT, g * T + t + 1)
                            mm(ps_wh[0], hT[0][:, :], wcat[g][:, :], start=True, stop=True).then_inc(d_whp, 1)
                    with pe.Fori(0, T) as t:
                        with pe.Fori(0, T // 4) as gr:
                            now = (n * T + t) * (T // 4) + gr + 1
                            pe.wait_ge(d_zs, now)
                            for c in range(4):
                                tr = nc.tensor.transpose(ps_z[:, c * P:(c + 1) * P], zs[:, c * P:(c + 1) * P], ident[:, :])
                            tr.then_inc(d_zTp, 1)
                            pe.wait_ge(d_zT, now)
                            for c in range(4):
                                last = mm(ps_o, zT[:, c * P:(c + 1) * P],
                                          H[:, bass.ds(gr * 4 + c, 1), 0:F].rearrange("p a f -> p (a f)"),
                                          start=c == 0, stop=c == 3)
                            last.then_inc(d_op, 1)
            with pe.Else():
                for q, w in weights.items():
                    with pe.Fori(0, T // 2) as u:
                        for i in range(2):
                            project(T * q, T * (q // 2), w, 2 * u + i, i)
                    pe.wait_ge(whsum_ready, w + 1)
                    mm(ps_small[:, 0:F], ones[:, :], whsum[:, 0:F], start=True, stop=True).then_inc(mean_psum, 1)


_INS = ["x", "adj", "L0_gnn_W", "L0_gnn_a", "L1_gnn_W", "L1_gnn_a", "L3_gnn_weight_w", "L3_gnn_weight_a", "L3_gnn_bias"]


def kernel(**inputs):
    import numpy as np
    import concourse.bacc as bacc
    from concourse.bass_utils import run_bass_kernel_spmd

    nc = bacc.Bacc("TRN2", target_bir_lowering=False, num_devices=1)
    arrays, args = {}, []
    for name in _INS:
        a = np.ascontiguousarray(inputs[name])
        arrays[f"in_{name}"] = a
        args.append(nc.dram_tensor(f"in_{name}", a.shape, mybir.dt.from_np(a.dtype), kind="ExternalInput").ap())
    out = nc.dram_tensor("out_x", (N, F), f32, kind="ExternalOutput").ap()
    build(nc, *args, out)
    r = run_bass_kernel_spmd(nc, [arrays], core_ids=[0])
    return r.results[0]["out_x"]
```
